# Optimizing a Trainium2 kernel written in Bass

```python
import numpy as np
import jax
import jax.numpy as jnp

def _softmax(x, axis=-1):
    return jax.nn.softmax(x, axis=axis)

def _gelu(x):
    return jax.nn.gelu(x, approximate=True)

def _silu(x):
    return jax.nn.silu(x)

def _sigmoid(x):
    return jax.nn.sigmoid(x)

def _layernorm(x, axis=-1, eps=1e-05):
    m = jnp.mean(x, axis=axis, keepdims=True)
    v = jnp.var(x, axis=axis, keepdims=True)
    return (x - m) / jnp.sqrt(v + eps)

def _scatter_add(tgt, idx, src, axis=0):
    return tgt.at[idx].add(src)

def _segment_sum(src, seg, n):
    return jax.ops.segment_sum(src, seg, n)
kernel_name = 'mk_gps_d1_gnn_r64_01d85c'

def setup_inputs(seed: int=0):
    np.random.seed(seed)
    _w = jnp.asarray

    def _rec_inputs():
        import jax
        import jax.numpy as jnp
        _gk = jax.random.key(seed)
        x = -0.0001074 + 0.9999 * jax.random.normal(jax.random.fold_in(_gk, 1), (50000, 256), jnp.float32)
        src = jax.random.randint(jax.random.fold_in(_gk, 2), (12500,), 0, 50000, jnp.int32)
        dst = jax.random.randint(jax.random.fold_in(_gk, 3), (12500,), 0, 50000, jnp.int32)
        _o = jnp.argsort(dst, stable=True)
        src = src[_o]
        dst = dst[_o]
        edge_attr_64 = -8.4373e-05 + 1.00001 * jax.random.normal(jax.random.fold_in(_gk, 12), (12500, 64), jnp.float32)
        edge_weight = jax.random.uniform(jax.random.fold_in(_gk, 13), (12500,), jnp.float32, 0.0, 0.999998)
        node_type_100 = jax.random.randint(jax.random.fold_in(_gk, 14), (50000,), 0, 100, jnp.int32)
        return (x, src, dst, edge_attr_64, edge_weight, node_type_100)
    x, src, dst, edge_attr_64, edge_weight, node_type_100 = _rec_inputs()

    def _L0_gnn_setup():
        import jax, jax.numpy as jnp
        import numpy as np
        N = 50000
        E = 12500
        C = 256
        RBF = 64
        NUM_SPECIES = 100
        CUTOFF = 5.0
        key = jax.random.key(seed)
        ks = jax.random.split(key, 10)
        node_z = jax.random.randint(ks[0], (N,), 0, NUM_SPECIES)
        node_feats = jax.random.normal(ks[1], (N, C), dtype=jnp.float32)
        senders = jax.random.randint(ks[2], (E,), 0, N)
        receivers = jnp.sort(jax.random.randint(ks[3], (E,), 0, N))
        edge_weight = jax.random.uniform(ks[4], (E,), dtype=jnp.float32)
        edge_feats = jax.random.normal(ks[5], (E, RBF), dtype=jnp.float32)
        embed_table = jax.random.normal(ks[6], (NUM_SPECIES, C), dtype=jnp.float32)
        lim_dp = float(np.sqrt(6.0 / (RBF + C)))
        W_dist = jax.random.uniform(ks[7], (RBF, C), minval=-lim_dp, maxval=lim_dp, dtype=jnp.float32)
        b_dist = jnp.zeros((C,), dtype=jnp.float32)
        lim_cb = float(np.sqrt(6.0 / (2 * C + C)))
        W_comb = jax.random.uniform(ks[8], (2 * C, C), minval=-lim_cb, maxval=lim_cb, dtype=jnp.float32)
        b_comb = jnp.zeros((C,), dtype=jnp.float32)
        return {'node_z': node_z, 'node_feats': node_feats, 'senders': senders, 'receivers': receivers, 'edge_weight': edge_weight, 'edge_feats': edge_feats, 'embed_table': embed_table, 'W_dist': W_dist, 'b_dist': b_dist, 'W_comb': W_comb, 'b_comb': b_comb}
    _L0_gnn_all = _L0_gnn_setup()
    _L0_gnn_in = {k: v for k, v in _L0_gnn_all.items() if k in ('embed_table', 'W_dist', 'b_dist', 'W_comb', 'b_comb')}
    del _L0_gnn_all

    def _L0_mix_setup():
        import jax, jax.numpy as jnp
        import numpy as np
        DIM = 256
        HEADS = 4
        DIM_HEAD = 32
        NUM_MEM = 4
        HIDDEN = HEADS * DIM_HEAD
        SCALE = DIM_HEAD ** (-0.5)

        def rmsnorm(x, g):
            n = jnp.linalg.norm(x, axis=-1, keepdims=True)
            return x / jnp.maximum(n, 1e-12) * g * x.shape[-1] ** 0.5
        key = jax.random.key(seed)
        ks = jax.random.split(key, 8)
        B, N = (4, 256)
        return {'x': jax.random.normal(ks[0], (B, N, DIM), jnp.float32), 't': jax.random.normal(ks[1], (B,), jnp.float32), 'w_qkv': jax.random.normal(ks[2], (DIM, 3 * HIDDEN), jnp.float32) * 0.02, 'mem_kv': jax.random.normal(ks[3], (2, HEADS, DIM_HEAD, NUM_MEM), jnp.float32), 'w_out': jax.random.normal(ks[4], (HIDDEN, DIM), jnp.float32) * 0.02, 'b_out': jnp.zeros((DIM,), jnp.float32), 'g_out': jnp.ones((DIM,), jnp.float32), 'g_pre': jnp.ones((DIM,), jnp.float32)}
    _L0_mix_all = _L0_mix_setup()
    _L0_mix_in = {k: v for k, v in _L0_mix_all.items() if k in ('t', 'w_qkv', 'mem_kv', 'w_out', 'b_out', 'g_out', 'g_pre')}
    del _L0_mix_all

    def _L0_ffn_setup():
        import jax, jax.numpy as jnp
        import numpy as np
        B, S, D = (8, 64, 256)
        H = 4 * D
        CAPACITY = 0.5
        key = jax.random.key(seed)
        ks = jax.random.split(key, 6)
        x = jax.random.normal(ks[0], (B, S, D), dtype=jnp.float32)
        attention_mask = jnp.zeros((B, 1, 1, S), dtype=jnp.float32)
        wr = jax.random.normal(ks[1], (D, 1), dtype=jnp.float32) * 0.02
        br = jnp.zeros((1,), dtype=jnp.float32)
        w1 = jax.random.normal(ks[2], (D, H), dtype=jnp.float32) * 0.02
        b1 = jnp.zeros((H,), dtype=jnp.float32)
        w2 = jax.random.normal(ks[3], (H, D), dtype=jnp.float32) * 0.02
        b2 = jnp.zeros((D,), dtype=jnp.float32)
        return {'x': x, 'attention_mask': attention_mask, 'wr': wr, 'br': br, 'w1': w1, 'b1': b1, 'w2': w2, 'b2': b2}
    _L0_ffn_all = _L0_ffn_setup()
    _L0_ffn_in = {k: v for k, v in _L0_ffn_all.items() if k in ('attention_mask', 'wr', 'br', 'w1', 'b1', 'w2', 'b2')}
    del _L0_ffn_all
    return {'x': x, 'src': src, 'dst': dst, 'edge_attr_64': edge_attr_64, 'edge_weight': edge_weight, 'node_type_100': node_type_100, 'L0_gnn_embed_table': _L0_gnn_in['embed_table'], 'L0_gnn_W_dist': _L0_gnn_in['W_dist'], 'L0_gnn_b_dist': _L0_gnn_in['b_dist'], 'L0_gnn_W_comb': _L0_gnn_in['W_comb'], 'L0_gnn_b_comb': _L0_gnn_in['b_comb'], 'L0_mix_t': _L0_mix_in['t'], 'L0_mix_w_qkv': _L0_mix_in['w_qkv'], 'L0_mix_mem_kv': _L0_mix_in['mem_kv'], 'L0_mix_w_out': _L0_mix_in['w_out'], 'L0_mix_b_out': _L0_mix_in['b_out'], 'L0_mix_g_out': _L0_mix_in['g_out'], 'L0_mix_g_pre': _L0_mix_in['g_pre'], 'L0_ffn_attention_mask': _L0_ffn_in['attention_mask'], 'L0_ffn_wr': _L0_ffn_in['wr'], 'L0_ffn_br': _L0_ffn_in['br'], 'L0_ffn_w1': _L0_ffn_in['w1'], 'L0_ffn_b1': _L0_ffn_in['b1'], 'L0_ffn_w2': _L0_ffn_in['w2'], 'L0_ffn_b2': _L0_ffn_in['b2']}

def reference(x, src, dst, edge_attr_64, edge_weight, node_type_100, L0_gnn_embed_table, L0_gnn_W_dist, L0_gnn_b_dist, L0_gnn_W_comb, L0_gnn_b_comb, L0_mix_t, L0_mix_w_qkv, L0_mix_mem_kv, L0_mix_w_out, L0_mix_b_out, L0_mix_g_out, L0_mix_g_pre, L0_ffn_attention_mask, L0_ffn_wr, L0_ffn_br, L0_ffn_w1, L0_ffn_b1, L0_ffn_w2, L0_ffn_b2):
    import jax
    import jax.numpy as jnp

    def _L0_gnn_ref(node_z, node_feats, senders, receivers, edge_weight, edge_feats, embed_table, W_dist, b_dist, W_comb, b_comb):
        import jax, jax.numpy as jnp
        import numpy as np
        N = 50000
        E = 12500
        C = 256
        RBF = 64
        NUM_SPECIES = 100
        CUTOFF = 5.0
        cut = 0.5 * (jnp.cos(edge_weight * jnp.pi / CUTOFF) + 1.0)
        cut = cut * (edge_weight < CUTOFF).astype(jnp.float32)
        W = (edge_feats @ W_dist + b_dist) * cut[:, None]
        x_j = embed_table[node_z][senders]
        msgs = x_j * W
        agg = jax.ops.segment_sum(msgs, receivers, num_segments=node_feats.shape[0])
        out = jnp.concatenate([node_feats, agg], axis=1) @ W_comb + b_comb
        return out

    def _L0_mix_ref(x, t, w_qkv, mem_kv, w_out, b_out, g_out, g_pre):
        import jax, jax.numpy as jnp
        import numpy as np
        DIM = 256
        HEADS = 4
        DIM_HEAD = 32
        NUM_MEM = 4
        HIDDEN = HEADS * DIM_HEAD
        SCALE = DIM_HEAD ** (-0.5)

        def rmsnorm(x, g):
            n = jnp.linalg.norm(x, axis=-1, keepdims=True)
            return x / jnp.maximum(n, 1e-12) * g * x.shape[-1] ** 0.5
        b, n, c = x.shape
        xn = rmsnorm(x, g_pre)
        qkv = xn @ w_qkv
        q, k, v = jnp.split(qkv, 3, axis=-1)

        def to_heads(z):
            return z.reshape(b, n, HEADS, DIM_HEAD).transpose(0, 2, 3, 1)
        q, k, v = map(to_heads, (q, k, v))
        mk = jnp.broadcast_to(mem_kv[0], (b, HEADS, DIM_HEAD, NUM_MEM))
        mv = jnp.broadcast_to(mem_kv[1], (b, HEADS, DIM_HEAD, NUM_MEM))
        k = jnp.concatenate([mk, k], axis=-1)
        v = jnp.concatenate([mv, v], axis=-1)
        q = jax.nn.softmax(q, axis=-2) * SCALE
        k = jax.nn.softmax(k, axis=-1)
        context = jnp.einsum('bhdn,bhen->bhde', k, v)
        out = jnp.einsum('bhde,bhdn->bhen', context, q)
        out = out.transpose(0, 3, 1, 2).reshape(b, n, HIDDEN)
        out = rmsnorm(out @ w_out + b_out, g_out)
        return out + x

    def _L0_ffn_ref(x, attention_mask, wr, br, w1, b1, w2, b2):
        import jax, jax.numpy as jnp
        import numpy as np
        B, S, D = (8, 64, 256)
        H = 4 * D
        CAPACITY = 0.5
        b, s, d = x.shape
        weights = (jnp.einsum('bsd,do->bso', x, wr) + br)[..., 0]
        k = max(1, int(CAPACITY * s))
        kk = k - 1 if k > 1 else 1
        _, idx = jax.lax.top_k(weights, k)
        sel_idx = idx[:, :kk]
        sel = jnp.take_along_axis(x, sel_idx[:, :, None], axis=1)
        h = jax.nn.gelu(jnp.einsum('bkd,dh->bkh', sel, w1) + b1)
        y = jnp.einsum('bkh,hd->bkd', h, w2) + b2
        w_sel = jnp.take_along_axis(weights, sel_idx, axis=1)
        y = y * w_sel[..., None]
        batch_idx = jnp.arange(b)[:, None]
        processed = jnp.zeros_like(x).at[batch_idx, sel_idx].set(y)
        return processed + x
    xn = _layernorm(x, axis=-1)
    x = x + _L0_gnn_ref(node_type_100, xn, src, dst, edge_weight, edge_attr_64, L0_gnn_embed_table, L0_gnn_W_dist, L0_gnn_b_dist, L0_gnn_W_comb, L0_gnn_b_comb) + _L0_mix_ref(xn[None], L0_mix_t, L0_mix_w_qkv, L0_mix_mem_kv, L0_mix_w_out, L0_mix_b_out, L0_mix_g_out, L0_mix_g_pre)[0]
    x = x + _L0_ffn_ref(_layernorm(x, axis=-1)[None], L0_ffn_attention_mask, L0_ffn_wr, L0_ffn_br, L0_ffn_w1, L0_ffn_b1, L0_ffn_w2, L0_ffn_b2)[0]
    return x

_drawn_inputs = setup_inputs


def setup_inputs(seed=0):
    import zlib

    import numpy as np

    out = dict(_drawn_inputs(seed))
    spreads = {'L0_gnn_b_dist': (0.0, 0.511),
     'L0_gnn_b_comb': (0.0, 0.1),
     'L0_mix_b_out': (0.0, 0.1),
     'L0_mix_g_out': (1.0, 0.2),
     'L0_mix_g_pre': (1.0, 0.6),
     'L0_ffn_b1': (0.0, 0.8),
     'L0_ffn_b2': (0.0, 0.8)}
    factors = {'edge_weight': 8.0,
     'L0_mix_w_qkv': 8.0,
     'L0_mix_mem_kv': 8.0,
     'L0_mix_w_out': 8.0,
     'L0_ffn_wr': 7.31,
     'L0_ffn_w1': 8.0,
     'L0_ffn_w2': 8.0}
    for name, (base, spread) in spreads.items():
        noise = np.random.default_rng([zlib.crc32(name.encode()), seed]).standard_normal(out[name].shape)
        drawn = base * np.exp(spread * noise) if base else spread * noise
        out[name] = jnp.asarray(drawn.astype(out[name].dtype))
    for name, factor in factors.items():
        out[name] = (out[name] * factor).astype(out[name].dtype)
    return out
```

```python
from contextlib import ExitStack

import numpy as np

import concourse.bass as bass
from concourse import mybir

F32 = mybir.dt.float32
BF16 = mybir.dt.bfloat16
I32 = mybir.dt.int32
ALU = mybir.AluOpType
ACT = mybir.ActivationFunctionType
AX = mybir.AxisListType

P = 128
J = 4
BLOCK = P * J
LN_EPS = 1e-5
RMS_FLOOR = 1e-12
CUTOFF = 5.0
FAR = float(1 << 20)
LOWEST = -3.0e38


class Step:

    def __init__(self, i, base):
        self.i, self.base = i, base

    def __add__(self, k):
        return Step(self.i, self.base + k)

    def __sub__(self, k):
        return Step(self.i, self.base - k)

    def of(self, scale, per):
        here = self.base // per * scale
        return here if self.i is None else self.i * (4 // per * scale) + here

    @property
    def n(self):
        return self.of(1, 1)

    def ring(self, k):
        return self.base % k

    def within(self, count):
        return self.i is not None or 0 <= self.base < count

    def is_last(self, count):
        return self.i is None and self.base == count - 1


def run_steps(eng, first, last, loop_from, loop_to, body):
    for n in range(first, loop_from):
        body(Step(None, n))
    with eng.Fori(0, (loop_to - loop_from) // 4) as i:
        for v in range(4):
            body(Step(i, loop_from + v))
    for n in range(loop_to, last + 1):
        body(Step(None, n))


def graph_layer(nc, a, out):
    x_d = a["x"]
    N, C = x_d.shape
    E = a["src"].shape[0]
    RBF = a["edge_attr_64"].shape[1]
    HID = a["L0_mix_w_out"].shape[0]
    HEADS = a["L0_mix_mem_kv"].shape[1]
    DH = HID // HEADS
    MEM = a["L0_mix_mem_kv"].shape[3]
    SPECIES = a["L0_gnn_embed_table"].shape[0]
    FF = a["L0_ffn_w1"].shape[1]
    NB = -(-N // BLOCK)
    COLS = NB * J
    TAIL = (N - (NB - 1) * BLOCK) // J
    NT = -(-E // P)
    assert C == 2 * P and HID == P and N % J == 0 and 0 < TAIL < P and NT == NB and NB % 2 == 0
    FULL_LANES, LAST_LANE = E // NT, E % NT
    K_SEL = N // 2 - 1
    NC = -(-K_SEL // BLOCK)
    LISTED = NC * J
    SLOTS = E + 1
    TABLE = -(-(SLOTS + P) // P) * P
    FK = FF // P
    REL = J + 1
    HI_LO = ((0, 0), (1, 0), (0, 1))

    ctx = ExitStack()
    with ctx:
        def sb(name, shape, dt=F32):
            return ctx.enter_context(nc.sbuf_tensor(name, shape, dt))

        def sem(name):
            return ctx.enter_context(nc.semaphore(name))

        ident = sb("ident", [P, P])
        ones = sb("ones", [P, P])
        ones_b = sb("ones_b", [P, P], BF16)
        bias_tmp = sb("bias_tmp", [P, C], BF16)
        before = sb("before", [P, P])
        earlier = sb("earlier", [P, P])
        same_head = sb("same_head", [P, P])
        iota_c = sb("iota_c", [P, max(COLS, LISTED, P)])
        lane_id = sb("lane_id", [P, 1])
        spare_row = sb("spare_row", [P, 1])
        half_neg = sb("half_neg", [P, 16])
        wk_s = sb("wk_s", [P, 2, 2, P], BF16)
        wq_s = sb("wq_s", [P, 2, 2, P], BF16)
        wc_s = sb("wc_s", [P, 2, 2, C], BF16)
        w1_s = sb("w1_s", [P, 2, 2, FF], BF16)
        w2_s = sb("w2_s", [P, 2, FK, C], BF16)
        wv_f = sb("wv_f", [P, 2, P])
        wb_f = sb("wb_f", [P, 2, C])
        wd_f = sb("wd_f", [RBF + 1, C])
        wo_f = sb("wo_f", [P, C])
        bias_b = sb("bias_b", [P, 3, C], BF16)
        b1_c = sb("b1_c", [P, FK])
        gout_r = sb("gout_r", [P, C])
        wr_r = sb("wr_r", [P, C])
        br_c = sb("br_c", [P, 1])
        wr_sum = sb("wr_sum", [P, 1])
        mem_k = sb("mem_k", [P, MEM])
        mem_v = sb("mem_v", [P, MEM])
        g_f = sb("g_f", [P, C])
        inv_sd = sb("inv_sd", [P, COLS])
        inv_rms = sb("inv_rms", [P, COLS])
        shift = sb("shift", [P, COLS])
        agg_row = sb("agg_row", [P, COLS], I32)
        stat2 = sb("stat2", [P, COLS, 4])
        dot2 = sb("dot2", [P, COLS])
        small = sb("small", [P, 64])
        small_i = sb("small_i", [P, 8], I32)

        AREA = 35000
        area = sb("area", [P, AREA])

        class Layout:
            def __init__(self):
                self.at = 0

            def __call__(self, *dims, dt=F32):
                size = int(np.prod(dims))
                words = size // 2 if dt == BF16 else size
                v = area[:, self.at:self.at + words]
                self.at += words
                assert self.at <= AREA, self.at
                if dt != F32:
                    v = v.bitcast(dt)
                names = " ".join(f"d{k}" for k in range(len(dims)))
                kw = {f"d{k}": dims[k] for k in range(len(dims))}
                return v.rearrange(f"p ({names}) -> p {names}", **kw) if len(dims) > 1 else v

        la = Layout()
        x_r = la(4, J, C)
        xr = la(4, J, C)
        xs_a = la(2, 2, 2, BLOCK, dt=BF16)
        e_t = la(2, BLOCK)
        e_n = la(2, BLOCK)
        bn = la(8, 6)
        pair = la(2, 12, 8)
        pow_in = la(2, 2, 8)
        pow_out = la(2, 2, 8)
        run_max = la(4)
        neg_max = la(4)
        blk_max = la(4)
        decay = la(4)
        row_sum = la(4)
        denom = la(1)
        acc = la(C)
        attr = la(NT, RBF)
        ends = la(2, NT, dt=I32)
        dst_f = la(NT)
        dst_p = la(NT)
        dst_c = la(NT)
        ei = la(3, NT, dt=I32)
        cut = la(NT)
        cut2 = la(NT)
        hot_p = la(2, P, dt=BF16)
        hot_c = la(2, COLS, dt=BF16)
        zero = la(C)
        count = la(COLS)
        touched = la(COLS)
        rank = la(COLS)
        rk = la(3, NB)
        slot_i = la(COLS, dt=I32)
        end_c = la(4, 2, dt=I32)
        kind_c = la(4, dt=I32)
        slot_c = la(4, dt=I32)
        goal = la(4, dt=I32)
        emb = la(4, C)
        attr_c = la(2, P)
        attr_t = la(2, P)
        diag = la(2, P)
        equal = la(2, P)
        junk_p = la(P)
        lead = la(2, 4)
        msg = la(2, C)
        msg_t = la(2, C)
        contrib = la(2, C)
        st_qkv = la(2, 3 * P)
        st_comb = la(2, C)
        g_pre = la(2)
        st_bias = la(3, C)
        sp_bias = la(2, C)
        top_a = la.at
        st_w1 = la(2, FF)
        st_w2 = la(FK, C)
        acc_t = la(2, P)
        mem_e = la(MEM)
        mem_t = la(2, P)
        ctx_t = la(P)

        lb = Layout()
        lb(4, J, C)
        xn = lb(2, J, C)
        s_b = lb(4, J, C)
        ag = lb(2, J, C)
        xs_b = lb(2, 2, 2, BLOCK, dt=BF16)
        q_e = lb(2, BLOCK)
        q_t = lb(2, BLOCK)
        q_max = lb(2, 16)
        q_sum = lb(2, 16)
        q_inv = lb(2, 16)
        sq_junk = lb(J, C)
        dot_junk = lb(J, C)
        sumsq = lb(4, J)
        mix_r = lb(4, 4, J)
        x1 = lb(4, J, C)
        o_b = lb(2, J, C)
        bn_b = lb(J, 6)
        ln_b = lb(2, 8, J)
        powb_in = lb(2, 2, J)
        powb_out = lb(2, 2, J)
        idx_b = lb(4, J, dt=I32)

        lt = Layout()
        w_all = lt(COLS)
        t_cmp = lt(COLS)
        t_gt = lt(COLS)
        t_eq = lt(COLS)
        t_sel = lt(COLS)
        t_rank = lt(COLS)
        t_rk = lt(3, NB)
        t_ri = lt(3, COLS, dt=I32)
        t_lane = lt(COLS)
        t_rel = lt(COLS)
        t_first = lt(NB)
        t_fi = lt(NB, dt=I32)
        j_pat = lt(COLS)
        hot5 = lt(COLS, 3, REL, dt=BF16)
        hot_l = lt(4, J, P, dt=BF16)
        iota_b = lt(P, dt=BF16)
        part = lt(REL, NB)
        part2 = lt(REL, NB)
        blk512 = lt(NB)
        part_t = lt(REL, P)
        first_c = lt(1)
        place = lt(REL, LISTED)
        pad_far = lt(LISTED)

        lc = Layout()
        listed = lc(LISTED, dt=I32)
        row_c = lc(4, J, dt=I32)
        g_r = lc(4, J, C)
        par = lc(4, J, 4)
        ln_c = lc(2, J, C)
        xs_c = lc(2, 2, 2, BLOCK, dt=BF16)
        h_f = lc(4, BLOCK)
        h_s = lc(2, 2, FK, BLOCK, dt=BF16)
        list_keep = sb("list_keep", [P, LISTED], I32)

        slot_tab = nc.dram_tensor("slot_tab", [NB * BLOCK, 1], I32, kind="Internal").ap()
        agg_tab = nc.dram_tensor("agg_tab", [TABLE, C], F32, kind="Internal").ap()
        row_tab = nc.dram_tensor("row_tab", [NB * BLOCK, 4], F32, kind="Internal").ap()

        psum = [ctx.enter_context(nc.psum_tensor(f"bank{k}", [P, 512], F32)) for k in range(8)]

        constants_ready = sem("constants_ready")
        pool_init = sem("pool_init")
        dve_init = sem("dve_init")
        weights_in = sem("weights_in")
        edges_in = sem("edges_in")
        table_zeroed = sem("table_zeroed")
        weights_ready = sem("weights_ready")
        edge_prep = sem("edge_prep")
        angle_ready = sem("angle_ready")
        cos_ready = sem("cos_ready")
        hot_ready = sem("hot_ready")
        hot_used = sem("hot_used")
        counted = sem("counted")
        rank_in = sem("rank_in")
        rank_sums = sem("rank_sums")
        rank_step = sem("rank_step")
        slots_ready = sem("slots_ready")
        slots_stored = sem("slots_stored")
        x_in = [sem(f"x_in{k}") for k in range(4)]
        stats_step = sem("stats_step")
        pow_in_ready = sem("pow_in_ready")
        pow_ready = sem("pow_ready")
        scale_step = sem("scale_step")
        normed = sem("normed")
        xt_ready = sem("xt_ready")
        xhi_ready = sem("xhi_ready")
        xlo_ready = sem("xlo_ready")
        keys_ready = sem("keys_ready")
        max_step = sem("max_step")
        exp_ready = sem("exp_ready")
        et_ready = sem("et_ready")
        en_ready = sem("en_ready")
        sums_ready = sem("sums_ready")
        acc_step = sem("acc_step")
        ends_ready = sem("ends_ready")
        kinds_in = [sem(f"kinds_in{k}") for k in range(4)]
        slots_in = [sem(f"slots_in{k}") for k in range(4)]
        emb_in = [sem(f"emb_in{k}") for k in range(4)]
        edge_cols = sem("edge_cols")
        attr_tr = sem("attr_tr")
        attr_t_ready = sem("attr_t_ready")
        dst_row = sem("dst_row")
        filter_ready = sem("filter_ready")
        equal_ready = sem("equal_ready")
        lead_step = sem("lead_step")
        msg_ready = sem("msg_ready")
        merged = sem("merged")
        merged_t = sem("merged_t")
        contrib_ps = sem("contrib_ps")
        contrib_ready = sem("contrib_ready")
        added = sem("added")
        stage_a_done = sem("stage_a_done")
        g_step = sem("g_step")
        g_ps = sem("g_ps")
        g_act = sem("g_act")
        g_ready = sem("g_ready")
        xb_in = [sem(f"xb_in{k}") for k in range(4)]
        xn_ready = sem("xn_ready")
        idx_ready = sem("idx_ready")
        ag_zero = sem("ag_zero")
        ag_in = [sem(f"ag_in{k}") for k in range(2)]
        s_ready = sem("s_ready")
        xbt_ready = sem("xbt_ready")
        bhi_ready = sem("bhi_ready")
        blo_ready = sem("blo_ready")
        q_ready = sem("q_ready")
        comb_ready = sem("comb_ready")
        qmax_step = sem("qmax_step")
        q_exp = sem("q_exp")
        q_sums = sem("q_sums")
        q_scaled = sem("q_scaled")
        qt_ps = sem("qt_ps")
        qt_ready = sem("qt_ready")
        mix_ready = sem("mix_ready")
        sumsq_ready = sem("sumsq_ready")
        powb_in_ready = sem("powb_in_ready")
        powb_ready = sem("powb_ready")
        factors_ready = sem("factors_ready")
        mix_used = sem("mix_used")
        u_ready = sem("u_ready")
        x1_ready = sem("x1_ready")
        ln_step = sem("ln_step")
        o_ready = sem("o_ready")
        o_stored = [sem(f"o_stored{k}") for k in range(2)]
        t_step = sem("t_step")
        t_counts = sem("t_counts")
        t_total = sem("t_total")
        params_ready = sem("params_ready")
        params_stored = sem("params_stored")
        hot5_ready = sem("hot5_ready")
        hotl_ready = sem("hotl_ready")
        hotl_used = sem("hotl_used")
        part_ready = sem("part_ready")
        part_tr = sem("part_tr")
        part_in = sem("part_in")
        list_ps = sem("list_ps")
        list_ready = sem("list_ready")
        cols_c = sem("cols_c")
        rows_in = [sem(f"rows_in{k}") for k in range(4)]
        pars_in = [sem(f"pars_in{k}") for k in range(4)]
        ln_ready = sem("ln_ready")
        ct_ready = sem("ct_ready")
        chi_ready = sem("chi_ready")
        clo_ready = sem("clo_ready")
        h_ps = sem("h_ps")
        h_act = sem("h_act")
        h_hi = sem("h_hi")
        h_lo = sem("h_lo")
        y_half = sem("y_half")
        y_ps = sem("y_ps")
        y_ready = sem("y_ready")
        scattered = [sem(f"scattered{k}") for k in range(4)]

        pool_count = nc.gpsimd.alloc_register("pool_count")

        def wait(eng, s, value):
            if isinstance(value, int):
                if value > 0:
                    eng.wait_ge(s, value)
            else:
                if eng is nc.gpsimd:
                    eng.reg_mov(pool_count, value)
                    eng.wait_ge(constants_ready, 1)
                    eng.wait_ge(s, pool_count)
                else:
                    eng.wait_ge(s, value)
                    eng.wait_ge(constants_ready, 1)

        def rows_of(s, count=NB):
            return TAIL if s.is_last(count) else P

        def x_block(t, s):
            n = rows_of(s)
            rows = s.n * BLOCK
            return t[bass.ds(rows, n * J), :].rearrange("(p j) c -> p j c", j=J)

        LOOP_A = (4, 4 + (NB - 6 - 4) // 4 * 4)
        LOOP_B = (8, 8 + (NB - 4 - 8) // 4 * 4)
        LAST_B = NB + 5
        LOOP_C = (4, 4 + (NC - 3 - 4) // 4 * 4)
        N_WEIGHTS = 21

        block = ctx.enter_context(nc.Block())

        @block.sync
        def _(sp):
            def load(dst, src, spread=False):
                sp.dma_start(dst, src, allow_slow_non_contiguous=spread).then_inc(weights_in, 16)

            sp.wait_ge(pool_init, 5)
            n_full = FULL_LANES * NT
            for k, name in enumerate(("dst", "src")):
                sp.dma_start(ends[0:FULL_LANES, k], a[name][0:n_full].rearrange("(p t) -> p t", t=NT)).then_inc(edges_in, 16)
                sp.dma_start(ends[FULL_LANES:FULL_LANES + 1, k, 0:LAST_LANE], a[name][n_full:E].rearrange("(p t) -> p t", p=1)).then_inc(edges_in, 16)
            sp.dma_start(cut[0:FULL_LANES, :], a["edge_weight"][0:n_full].rearrange("(p t) -> p t", t=NT)).then_inc(edges_in, 16)
            sp.dma_start(cut[FULL_LANES:FULL_LANES + 1, 0:LAST_LANE], a["edge_weight"][n_full:E].rearrange("(p t) -> p t", p=1)).then_inc(edges_in, 16)
            load(st_qkv, a["L0_mix_w_qkv"].rearrange("(k p) n -> p k n", p=P))
            load(g_pre, a["L0_mix_g_pre"].rearrange("(k p) -> p k", p=P), spread=True)
            load(st_comb, a["L0_gnn_W_comb"][0:C, :].rearrange("(k p) n -> p k n", p=P))
            load(wb_f[:], a["L0_gnn_W_comb"][C:2 * C, :].rearrange("(k p) n -> p k n", p=P))
            load(wd_f[0:RBF, :], a["L0_gnn_W_dist"])
            load(wd_f[RBF:RBF + 1, :], a["L0_gnn_b_dist"].rearrange("(o n) -> o n", o=1))
            load(wo_f[:], a["L0_mix_w_out"])
            for k, name in enumerate(("L0_gnn_b_comb", "L0_mix_b_out", "L0_ffn_b2")):
                load(st_bias[:, k, :], a[name].rearrange("(o n) -> o n", o=1).to_broadcast([P, C]))
            load(gout_r[:], a["L0_mix_g_out"].rearrange("(o n) -> o n", o=1).to_broadcast([P, C]))
            load(wr_r[:], a["L0_ffn_wr"].rearrange("n o -> o n").to_broadcast([P, C]))
            load(br_c[:], a["L0_ffn_br"].rearrange("(o n) -> o n", o=1).to_broadcast([P, 1]))
            load(b1_c[:], a["L0_ffn_b1"].rearrange("(m p) -> p m", p=P), spread=True)
            load(mem_k[:], a["L0_mix_mem_kv"][0].rearrange("h d m -> (h d) m"))
            load(mem_v[:], a["L0_mix_mem_kv"][1].rearrange("h d m -> (h d) m"))
            part112 = FULL_LANES // 16 * 16
            load(attr[0:part112], a["edge_attr_64"][0:part112 * NT, :].rearrange("(p t) c -> p t c", t=NT))
            load(attr[part112:FULL_LANES], a["edge_attr_64"][part112 * NT:n_full, :].rearrange("(p t) c -> p t c", t=NT))
            load(attr[FULL_LANES:FULL_LANES + 1, 0:LAST_LANE], a["edge_attr_64"][n_full:E, :].rearrange("(p t) c -> p t c", p=1))
            load(st_w1, a["L0_ffn_w1"].rearrange("(k p) n -> p k n", p=P))
            load(st_w2, a["L0_ffn_w2"].rearrange("(k p) n -> p k n", p=P))
            sp.dma_start(agg_tab.rearrange("(p r) c -> p r c", p=P), zero.unsqueeze(1).to_broadcast([P, TABLE // P, C])).then_inc(table_zeroed, 16)
            sp.wait_ge(slots_ready, 1)
            sp.dma_start(slot_tab.rearrange("(b p j) o -> p b (j o)", p=P, j=J), slot_i.rearrange("p (b j) -> p b j", j=J)).then_inc(slots_stored, 16)

            def load_a(s):
                if s.within(NB):
                    wait(sp, normed, (s - 3).n)
                    sp.dma_start(x_r[0:rows_of(s), s.ring(4)], x_block(x_d, s)).then_inc(x_in[s.ring(4)], 16)

            run_steps(sp, 0, NB - 1, *LOOP_A, load_a)

            sp.wait_ge(stage_a_done, 1)

            def traffic_b(s):
                ld, st = s + 3, s - 6
                if ld.within(NB):
                    wait(sp, u_ready, (ld - 3).n)
                    sp.dma_start(x_r[0:rows_of(ld), ld.ring(4)], x_block(x_d, ld)).then_inc(xb_in[ld.ring(4)], 16)
                if st.within(NB):
                    wait(sp, o_ready, (st + 1).n)
                    sp.dma_start(x_block(out, st), o_b[0:rows_of(st), st.ring(2)]).then_inc(o_stored[st.ring(2)], 16)

            run_steps(sp, -3, LAST_B, *LOOP_B, traffic_b)
            sp.wait_ge(params_ready, 1)
            sp.dma_start(row_tab.rearrange("(b p j) k -> p b (j k)", p=P, j=J), stat2[:].rearrange("p (b j) k -> p b (j k)", j=J)).then_inc(params_stored, 16)

        @block.gpsimd
        def _(pool):
            g = nc.gpsimd
            g.iota(ends[:, 0], pattern=[[0, NT]], base=N, channel_multiplier=0).then_inc(pool_init, 1)
            g.memset(cut, 0.0).then_inc(pool_init, 1)
            g.iota(ends[:, 1], pattern=[[0, NT]], base=0, channel_multiplier=0).then_inc(pool_init, 1)
            g.memset(attr, 0.0).then_inc(pool_init, 1)
            g.memset(zero, 0.0).then_inc(pool_init, 1)
            g.iota(iota_c[:], pattern=[[1, iota_c.shape[1]]], base=0, channel_multiplier=0, allow_small_or_imprecise_dtypes=True)
            g.iota(lane_id[:], pattern=[[0, 1]], base=0, channel_multiplier=1, allow_small_or_imprecise_dtypes=True)
            g.iota(spare_row[:], pattern=[[0, 1]], base=SLOTS, channel_multiplier=1, allow_small_or_imprecise_dtypes=True)
            g.memset(half_neg[:], -0.5)
            g.memset(ones_b[:], 1.0)
            g.memset(ones[:], 1.0).then_inc(constants_ready, 1)
            pool.wait_ge(constants_ready, 1)
            g.affine_select(out=ident[:], in_=ones[:], compare_op=ALU.is_equal, fill=0.0, base=0, pattern=[[-1, P]], channel_multiplier=1)
            g.affine_select(out=before[:], in_=ones[:], compare_op=ALU.is_gt, fill=0.0, base=0, pattern=[[1, P]], channel_multiplier=-1)
            g.affine_select(out=earlier[:], in_=ones[:], compare_op=ALU.is_gt, fill=0.0, base=0, pattern=[[-1, P]], channel_multiplier=1)
            g.affine_select(out=same_head[:].rearrange("p (h d) -> p h d", d=DH), in_=ones[:].rearrange("p (h d) -> p h d", d=DH),
                            compare_op=ALU.is_ge, fill=0.0, base=0, pattern=[[-DH, HEADS], [0, DH]], channel_multiplier=1).then_inc(constants_ready, 1)
            pool.wait_ge(constants_ready, 2)
            g.affine_select(out=same_head[:].rearrange("p (h d) -> p h d", d=DH), in_=same_head[:].rearrange("p (h d) -> p h d", d=DH),
                            compare_op=ALU.is_ge, fill=0.0, base=DH - 1, pattern=[[DH, HEADS], [0, DH]], channel_multiplier=-1).then_inc(constants_ready, 1)
            pool.wait_ge(slots_stored, 16)
            pool.wait_ge(table_zeroed, 16)

            def step_a(s):
                nxt = s + 2
                if nxt.ring(2) == 0 and nxt.within(NB):
                    k = nxt.ring(4) // 2
                    wait(pool, pow_in_ready, nxt.of(1, 2) + 1)
                    g.tensor_tensor(pow_out[:, k], pow_in[:, k], half_neg[:].rearrange("p (a b) -> p a b", a=2), ALU.pow).then_inc(pow_ready, 1)
                t = s + 2
                if t.within(NT):
                    k = t.ring(4)
                    wait(pool, ends_ready, t.n + 1)
                    wait(pool, emb_in[k], t.of(16, 4))
                    wait(pool, lead_step, (t - 3).of(4, 1))
                    g.indirect_dma_start(kind_c[:, k:k + 1], None, a["node_type_100"].rearrange("(n o) -> n o", o=1),
                                         bass.IndirectOffsetOnAxis(ap=end_c[:, k, 1:2], axis=0), bounds_check=N - 1, oob_is_err=False).then_inc(kinds_in[k], 16)
                    g.indirect_dma_start(slot_c[:, k:k + 1], None, slot_tab,
                                         bass.IndirectOffsetOnAxis(ap=end_c[:, k, 0:1], axis=0), bounds_check=NB * BLOCK - 1, oob_is_err=False).then_inc(slots_in[k], 16)
                t = s + 1
                if t.within(NT):
                    k = t.ring(4)
                    wait(pool, kinds_in[k], t.of(16, 4) + 16)
                    wait(pool, msg_ready, (t - 3).n)
                    g.indirect_dma_start(emb[:, k], None, a["L0_gnn_embed_table"],
                                         bass.IndirectOffsetOnAxis(ap=kind_c[:, k:k + 1], axis=0), bounds_check=SPECIES - 1, oob_is_err=False).then_inc(emb_in[k], 16)
                t = s - 2
                if t.within(NT):
                    wait(pool, contrib_ready, t.n + 1)
                    wait(pool, added, t.of(16, 1))
                    g.indirect_dma_start(agg_tab, bass.IndirectOffsetOnAxis(ap=goal[:, t.ring(4):t.ring(4) + 1], axis=0), contrib[:, t.ring(2)], None,
                                         bounds_check=TABLE - 1, compute_op=ALU.add).then_inc(added, 16)

            run_steps(pool, -2, NB + 1, *LOOP_A, step_a)
            pool.wait_ge(added, 16 * NT)
            pool.wait_ge(stage_a_done, 1)

            def step_b(s):
                t = s + 1
                if t.within(NB):
                    k = t.ring(2)
                    wait(pool, s_ready, (t - 1).n)
                    g.memset(ag[:, k], 0.0).then_inc(ag_zero, 1)
                    wait(pool, ag_zero, t.n + 1)
                    wait(pool, idx_ready, t.n + 1)
                    for j in range(J):
                        g.indirect_dma_start(ag[:, k, j], None, agg_tab, bass.IndirectOffsetOnAxis(ap=idx_b[:, t.ring(4), j:j + 1], axis=0),
                                             bounds_check=TABLE - 1, oob_is_err=False).then_inc(ag_in[k], 16)
                if s.within(NB):
                    n, k = rows_of(s), s.ring(2)
                    wait(pool, xn_ready, s.n + 1)
                    wait(pool, ag_in[k], s.of(16 * J, 2) + 16 * J)
                    g.tensor_tensor(x_r[0:n, s.ring(4)], x_r[0:n, s.ring(4)], ag[0:n, k], ALU.add).then_inc(s_ready, 1)
                t = s - 1
                if t.within(NB):
                    n, k = rows_of(t), t.ring(2)
                    wait(pool, q_sums, 2 * t.n + 2)
                    wait(pool, q_exp, t.n + 1)
                    v = q_e[0:n, k].rearrange("p (h d) -> p h d", d=DH)
                    g.tensor_tensor(v, v, q_inv[0:n, k].unsqueeze(2).to_broadcast([n, 16, DH]), ALU.mult).then_inc(q_scaled, 1)
                t = s - 3
                if t.within(NB + 2):
                    k = (t + 1).ring(2)
                    wait(pool, powb_in_ready, t.n + 1)
                    g.tensor_tensor(powb_out[:, k], powb_in[:, k], half_neg[:, 0:2 * J].rearrange("p (a b) -> p a b", a=2), ALU.pow).then_inc(powb_ready, 1)

            run_steps(pool, -1, LAST_B, *LOOP_B, step_b)

            pool.wait_ge(params_stored, 16)
            for k in range(2):
                pool.wait_ge(o_stored[k], 16 * (NB // 2))

            def step_c(s):
                t = s + 2
                if t.within(NC):
                    k = t.ring(4)
                    wait(pool, cols_c, t.n + 1)
                    wait(pool, scattered[k], t.of(16 * J, 4))
                    for j in range(J):
                        g.indirect_dma_start(g_r[:, k, j], None, out, bass.IndirectOffsetOnAxis(ap=row_c[:, k, j:j + 1], axis=0),
                                             bounds_check=N - 1, oob_is_err=False).then_inc(rows_in[k], 16)
                        g.indirect_dma_start(par[:, k, j], None, row_tab, bass.IndirectOffsetOnAxis(ap=row_c[:, k, j:j + 1], axis=0),
                                             bounds_check=N - 1, oob_is_err=False).then_inc(pars_in[k], 16)
                t = s - 1
                if t.within(NC):
                    k = t.ring(4)
                    wait(pool, y_ready, t.n + 1)
                    for j in range(J):
                        g.indirect_dma_start(out, bass.IndirectOffsetOnAxis(ap=row_c[:, k, j:j + 1], axis=0), g_r[:, k, j], None,
                                             bounds_check=N - 1, oob_is_err=False).then_inc(scattered[k], 16)

            run_steps(pool, -2, NC, *LOOP_C, step_c)
            for k in range(4):
                pool.wait_ge(scattered[k], 16 * J * len(range(k, NC, 4)))

        @block.scalar
        def _(act):
            sc = nc.scalar
            act.wait_ge(angle_ready, 1)
            sc.activation(cut2, cut2, ACT.Sin).then_inc(cos_ready, 1)

            def step_a(s):
                b = s - 2
                if b.within(NB):
                    n = rows_of(b)
                    wait(act, et_ready, b.n + 1)
                    wait(act, sums_ready, (b - 1).n)
                    sc.copy(e_n[0:n, b.ring(2)], psum[3][0:n, :]).then_inc(en_ready, 1)
                if s.within(NB):
                    n = rows_of(s)
                    wait(act, xt_ready, s.n + 1)
                    wait(act, keys_ready, (s - 1).n)
                    for k in range(2):
                        ins = sc.copy(xs_a[:, s.ring(2), 0, k].rearrange("p (j r) -> p j r", j=J)[:, :, 0:n],
                                      psum[k][:].rearrange("p (j r) -> p j r", j=J)[:, :, 0:n])
                    ins.then_inc(xhi_ready, 1)
                t = s
                if t.within(NT):
                    wait(act, attr_tr, t.n + 1)
                    wait(act, filter_ready, (t - 1).n)
                    sc.copy(attr_t[0:RBF, t.ring(2)], psum[5][0:RBF, 0:P]).then_inc(attr_t_ready, 1)
                b = s + 1
                if b.within(NB):
                    n, k4, h = rows_of(b), b.ring(4), b.ring(2) * J
                    pr = pair[:, k4 // 2]
                    wait(act, scale_step, b.of(5, 2) + 5)
                    wait(act, x_in[k4], b.of(16, 4) + 16)
                    wait(act, sums_ready, (b - 3).n)
                    for j in range(J):
                        ins = sc.activation(xr[0:n, k4, j], x_r[0:n, k4, j], ACT.Identity, scale=pr[0:n, 7, h + j:h + j + 1], bias=pr[0:n, 9, h + j:h + j + 1])
                    ins.then_inc(normed, 1)
                t = s - 1
                if t.within(NT):
                    wait(act, merged, t.n + 1)
                    sc.copy(msg_t[:, t.ring(2)], psum[6][:, 0:C]).then_inc(merged_t, 1)
                b = s - 1
                if b.within(NB):
                    w = rows_of(b) * J
                    k = b.ring(4)
                    wait(act, keys_ready, b.n + 1)
                    wait(act, max_step, 3 * b.n + 3)
                    wait(act, et_ready, (b - 1).n)
                    sc.activation(e_t[:, b.ring(2), 0:w], psum[2][:, 0:w], ACT.Exp, bias=neg_max[:, k:k + 1], accum_out=row_sum[:, k:k + 1])
                    sc.activation(decay[:, k:k + 1], run_max[:, (k - 1) % 4:(k - 1) % 4 + 1], ACT.Exp, bias=neg_max[:, k:k + 1]).then_inc(exp_ready, 1)
                t = s - 1
                if t.within(NT):
                    wait(act, contrib_ps, t.n + 1)
                    wait(act, added, (t - 1).of(16, 1))
                    sc.copy(contrib[:, t.ring(2)], psum[6][:, C:2 * C]).then_inc(contrib_ready, 1)

            run_steps(act, -1, NB + 1, *LOOP_A, step_a)

            act.wait_ge(g_step, 2)
            sc.activation(mem_e, mem_k[:], ACT.Exp, bias=neg_max[:, (NB - 1) % 4:(NB - 1) % 4 + 1], accum_out=small[:, 8:9]).then_inc(g_act, 1)

            def step_b(s):
                b = s - 3
                if b.within(NB):
                    n = rows_of(b)
                    wait(act, qt_ps, b.n + 1)
                    wait(act, mix_ready, (b - 1).n)
                    sc.copy(q_t[:, b.ring(2)].rearrange("p (j r) -> p j r", j=J)[:, :, 0:n], psum[3][:].rearrange("p (j r) -> p j r", j=J)[:, :, 0:n]).then_inc(qt_ready, 1)
                if s.within(NB):
                    n = rows_of(s)
                    wait(act, xbt_ready, s.n + 1)
                    wait(act, comb_ready, (s - 1).n)
                    for k in range(2):
                        ins = sc.copy(xs_b[:, s.ring(2), 0, k].rearrange("p (j r) -> p j r", j=J)[:, :, 0:n],
                                      psum[k][:].rearrange("p (j r) -> p j r", j=J)[:, :, 0:n])
                    ins.then_inc(bhi_ready, 1)
                b = s + 1
                if b.within(NB):
                    n, k = rows_of(b), b.ring(2)
                    wait(act, xb_in[b.ring(4)], b.of(16, 4) + 16)
                    wait(act, xbt_ready, (b - 1).n)
                    for j in range(J):
                        col = b.n * J + j
                        ins = sc.activation(xn[0:n, k, j], x_r[0:n, b.ring(4), j], ACT.Identity, scale=inv_sd[0:n, bass.ds(col, 1)], bias=shift[0:n, bass.ds(col, 1)])
                    ins.then_inc(xn_ready, 1)
                b = s - 1
                if b.within(NB):
                    n, k = rows_of(b), b.ring(2)
                    wait(act, qmax_step, 2 * b.n + 2)
                    for j in range(J):
                        col = b.n * J + j
                        ins = sc.activation(q_e[0:n, k, j * P:(j + 1) * P], q_e[0:n, k, j * P:(j + 1) * P], ACT.Exp,
                                            scale=inv_rms[0:n, bass.ds(col, 1)])
                    ins.then_inc(q_exp, 1)
                b = s - 3
                if b.within(NB):
                    n = rows_of(b)
                    wait(act, mix_ready, b.n + 1)
                    for j in range(J):
                        ins = sc.activation(sq_junk[0:n, j], psum[6 + j // 2][0:n, j % 2 * C:(j % 2 + 1) * C], ACT.Square,
                                            accum_out=sumsq[0:n, b.ring(4), j:j + 1])
                    ins.then_inc(sumsq_ready, 1)
                b = s - 6
                if b.within(NB):
                    n, k = rows_of(b), b.ring(2)
                    wait(act, factors_ready, b.n + 1)
                    wait(act, o_stored[k], b.of(16, 2))
                    for j in range(J):
                        ins = sc.activation(o_b[0:n, k, j], x1[0:n, b.ring(4), j], ACT.Identity, scale=mix_r[0:n, b.ring(4), 2, j:j + 1], bias=mix_r[0:n, b.ring(4), 3, j:j + 1])
                    ins.then_inc(o_ready, 1)

            run_steps(act, -1, LAST_B, *LOOP_B, step_b)

            def step_c(s):
                if s.within(NC):
                    for m in range(FK):
                        wait(act, h_ps, s.of(FK, 1) + m + 1)
                        wait(act, h_lo, s.of(FK, 1) + m - 3)
                        sc.activation(h_f[:, m % 4], psum[2 + m % 4][:], ACT.Gelu_apprx_tanh, bias=b1_c[:, m:m + 1]).then_inc(h_act, 1)
                b = s + 1
                if b.within(NC):
                    wait(act, ct_ready, b.n + 1)
                    wait(act, h_ps, (b - 1).of(FK, 1))
                    for k in range(2):
                        ins = sc.copy(xs_c[:, b.ring(2), 0, k], psum[k][:])
                    ins.then_inc(chi_ready, 1)

            run_steps(act, -1, NC - 1, *LOOP_C, step_c)

        @block.vector
        def _(dve):
            v = nc.vector

            def split(parts, whole, done=None):
                v.tensor_copy(parts[0], whole).then_inc(dve_init, 1)
                split.count += 1
                dve.wait_ge(dve_init, split.count)
                ins = v.tensor_tensor(parts[1], whole, parts[0], ALU.subtract)
                return ins

            split.count = 0

            def chain(ins):
                ins.then_inc(dve_init, 1)
                split.count += 1
                dve.wait_ge(dve_init, split.count)

            def ranks(mask, rank_out, tmp, turn):
                m3 = mask.rearrange("p (b j) -> p b j", j=J)
                r3 = rank_out.rearrange("p (b j) -> p b j", j=J)
                v.tensor_reduce(tmp[:, 0], m3, AX.X, ALU.add).then_inc(rank_in, 1)
                dve.wait_ge(rank_sums, turn)
                v.tensor_tensor_scan(tmp[:, 1], ones[:, 0:1].to_broadcast([P, NB]), psum[5][:, 0:NB], 0.0, ALU.mult, ALU.add).then_inc(rank_step, 1)
                dve.wait_ge(rank_step, 6 * turn - 5)
                v.tensor_tensor(tmp[:, 2], tmp[:, 1], psum[5][:, 0:NB], ALU.subtract).then_inc(rank_step, 1)
                dve.wait_ge(rank_step, 6 * turn - 4)
                v.tensor_tensor(r3[:, :, 0], tmp[:, 2], psum[4][:, 0:NB], ALU.add).then_inc(rank_step, 1)
                for j in range(1, J):
                    dve.wait_ge(rank_step, 6 * turn - 4 + j)
                    v.tensor_tensor(r3[:, :, j], r3[:, :, j - 1], m3[:, :, j - 1], ALU.add).then_inc(rank_step, 1)
                dve.wait_ge(rank_step, 6 * turn)

            v.memset(small[:], 0.0)
            v.memset(attr_t, 1.0)
            v.memset(attr_c, 0.0)
            v.memset(bn, 0.0)
            v.memset(acc, 0.0)
            v.memset(denom, 0.0)
            v.memset(inv_sd[:], 0.0)
            v.memset(inv_rms[:], 0.0)
            v.memset(shift[:], 0.0)
            v.memset(stat2[:], 0.0)
            chain(v.memset(dot2[:], 0.0))
            dve.wait_ge(constants_ready, 3)
            dve.wait_ge(edges_in, 96)
            chain(v.tensor_scalar(cut2, cut, -1.0, None, ALU.mult))
            chain(v.tensor_tensor(cut2, cut2, cut, ALU.max))
            chain(v.tensor_scalar(cut2, cut2, CUTOFF, -float(np.pi) / CUTOFF, ALU.min, ALU.mult))
            v.tensor_scalar(cut2, cut2, float(np.pi) / 2, None, ALU.add).then_inc(angle_ready, 1)
            chain(v.tensor_scalar(ei[:, 0], ends[:, 0], 2, 127, ALU.logical_shift_right, ALU.bitwise_and))
            chain(v.tensor_scalar(ei[:, 1], ends[:, 0], 9, 2, ALU.logical_shift_right, ALU.logical_shift_left))
            chain(v.tensor_scalar(ei[:, 2], ends[:, 0], 3, None, ALU.bitwise_and))
            chain(v.tensor_tensor(ei[:, 1], ei[:, 1], ei[:, 2], ALU.bitwise_or))
            v.tensor_copy(dst_f, ends[:, 0])
            v.tensor_copy(dst_p, ei[:, 0])
            chain(v.tensor_copy(dst_c, ei[:, 1]))

            def hot(t, k, used):
                if used is not None:
                    wait(dve, hot_used, used)
                v.tensor_scalar(hot_p[:, k], iota_c[:, 0:P], dst_p[:, bass.ds(t, 1)], None, ALU.is_equal)
                v.tensor_scalar(hot_c[:, k], iota_c[:, 0:COLS], dst_c[:, bass.ds(t, 1)], None, ALU.is_equal).then_inc(hot_ready, 1)

            hot(0, 0, None)
            hot(1, 1, None)
            with dve.Fori(0, NT // 2 - 1) as i:
                for k in range(2):
                    hot(i * 2 + (2 + k), k, i * 2 + (1 + k))
            dve.wait_ge(counted, 1)
            chain(v.tensor_scalar(touched, psum[7][:, 0:COLS], 0.5, None, ALU.is_gt))
            ranks(touched, rank, rk, 1)
            chain(v.tensor_scalar(count, rank, FAR, None, ALU.subtract))
            chain(v.tensor_tensor(count, count, touched, ALU.mult))
            v.tensor_scalar(agg_row[:], count, FAR, None, ALU.add)
            v.tensor_copy(slot_i, rank).then_inc(slots_ready, 1)

            dve.wait_ge(weights_in, 16 * N_WEIGHTS)
            for k in range(2):
                chain(v.tensor_scalar(st_qkv[:, k], st_qkv[:, k], g_pre[:, k:k + 1], None, ALU.mult))
            chain(v.tensor_copy(wv_f[:], st_qkv[:, :, 2 * P:3 * P]))
            chain(split([wq_s[:, 0], wq_s[:, 1]], st_qkv[:, :, 0:P]))
            chain(split([wk_s[:, 0], wk_s[:, 1]], st_qkv[:, :, P:2 * P]))
            for k in range(2):
                chain(v.tensor_tensor(st_comb[:, k, k * P:(k + 1) * P], st_comb[:, k, k * P:(k + 1) * P], ident[:], ALU.add))
            chain(split([wc_s[:, 0], wc_s[:, 1]], st_comb))
            chain(split([w1_s[:, 0], w1_s[:, 1]], st_w1))
            chain(split([w2_s[:, 0], w2_s[:, 1]], st_w2))
            v.memset(bias_b[96:128], 0.0)
            chain(v.tensor_scalar(st_bias, st_bias, 1.0 / 32, None, ALU.mult))
            chain(v.tensor_copy(bias_b[0:32], st_bias[0:32]))
            for k in range(3):
                chain(v.tensor_copy(bias_tmp[:], st_bias[:, k]))
                chain(v.tensor_tensor(sp_bias[:, 0], st_bias[:, k], bias_tmp[:], ALU.subtract))
                chain(v.tensor_copy(bias_b[32:64, k], sp_bias[32:64, 0]))
                chain(v.tensor_copy(bias_tmp[:], sp_bias[:, 0]))
                chain(v.tensor_tensor(sp_bias[:, 1], sp_bias[:, 0], bias_tmp[:], ALU.subtract))
                chain(v.tensor_copy(bias_b[64:96, k], sp_bias[64:96, 1]))
            chain(v.tensor_reduce(wr_sum[:], wr_r[:], AX.X, ALU.add))
            chain(v.tensor_reduce(run_max[:, 3:4], mem_k[:], AX.X, ALU.max))
            dve.wait_ge(cos_ready, 1)
            chain(v.tensor_scalar(cut2, cut2, 1.0, 0.5, ALU.add, ALU.mult))
            chain(v.tensor_scalar(cut, cut, CUTOFF, None, ALU.is_lt))
            v.tensor_tensor(cut2, cut2, cut, ALU.mult).then_inc(weights_ready, 1)
            dve.wait_ge(weights_ready, 1)

            def step_a(s):
                b = s - 3
                if b.within(NB):
                    kb = b.ring(4)
                    wait(dve, exp_ready, b.n + 1)
                    wait(dve, sums_ready, b.n + 1)
                    wait(dve, acc_step, b.n)
                    v.scalar_tensor_tensor(denom, denom, decay[:, kb:kb + 1], row_sum[:, kb:kb + 1], ALU.mult, ALU.add)
                    v.scalar_tensor_tensor(acc, acc, decay[:, kb:kb + 1], psum[4][:, 0:C], ALU.mult, ALU.add).then_inc(acc_step, 1)
                b = s - 1
                if b.within(NB):
                    w, kb = rows_of(b) * J, b.ring(4)
                    wait(dve, keys_ready, b.n + 1)
                    v.tensor_reduce(blk_max[:, kb:kb + 1], psum[2][:, 0:w], AX.X, ALU.max).then_inc(max_step, 1)
                t = s + 1
                if t.within(NT):
                    k = t.ring(2)
                    wait(dve, attr_tr, (t - 1).n)
                    wait(dve, dst_row, (t - 1).n)
                    v.tensor_copy(attr_c[:, k, 0:RBF], attr[:, bass.ds(t.n, 1), :])
                    v.tensor_scalar(diag[:, k], ident[:], dst_f[:, bass.ds(t.n, 1)], None, ALU.mult).then_inc(edge_cols, 1)
                if (s - 1).within(NB):
                    wait(dve, max_step, 3 * (s - 1).n + 1)
                    p_ = (kb - 1) % 4
                    v.tensor_tensor(run_max[:, kb:kb + 1], blk_max[:, kb:kb + 1], run_max[:, p_:p_ + 1], ALU.max).then_inc(max_step, 1)
                t = s + 3
                if t.within(NT):
                    wait(dve, kinds_in[t.ring(4)], t.of(16, 4))
                    wait(dve, slots_in[t.ring(4)], t.of(16, 4))
                    v.tensor_copy(end_c[:, t.ring(4)], ends[:, :, bass.ds(t.n, 1)].rearrange("p a o -> p (a o)")).then_inc(ends_ready, 1)
                if (s - 1).within(NB):
                    wait(dve, max_step, 3 * (s - 1).n + 2)
                    v.tensor_scalar(neg_max[:, kb:kb + 1], run_max[:, kb:kb + 1], -1.0, None, ALU.mult).then_inc(max_step, 1)
                b = s + 1
                first = b.ring(2) == 0 and b.within(NB)
                if first:
                    k, at, cols = b.ring(4) // 2, b.of(5, 2), bass.ds(b.n * J, 2 * J)
                    pr = pair[:, k]
                    wait(dve, pow_ready, b.of(1, 2) + 1)
                    wait(dve, normed, (b - 2).n)
                    v.tensor_tensor(pr[:, 7], pow_out[:, k, 0], pow_out[:, k, 1], ALU.mult)
                    v.scalar_tensor_tensor(pr[:, 8], pr[:, 0], -0.5, pow_out[:, k, 0], ALU.mult, ALU.mult).then_inc(scale_step, 1)
                    v.tensor_copy(inv_sd[:, cols], pow_out[:, k, 0])
                    v.tensor_copy(inv_rms[:, cols], pow_out[:, k, 1])
                    wait(dve, scale_step, at + 3)
                    v.tensor_tensor(pr[:, 9], pr[:, 8], pow_out[:, k, 1], ALU.mult).then_inc(scale_step, 1)
                    v.tensor_copy(shift[:, cols], pr[:, 8]).then_inc(scale_step, 1)
                q = s + 2
                stats = q.ring(2) == 0 and q.within(NB)
                if stats:
                    kq, at = q.ring(4) // 2, q.of(5, 2)
                    pq = pair[:, kq]
                    for h in range(2):
                        b = q + h
                        n = rows_of(b)
                        wait(dve, x_in[b.ring(4)], b.of(16, 4) + 16)
                        for j in range(J):
                            ins = v.bn_stats(bn[0:n, 4 * h + j], x_r[0:n, b.ring(4), j])
                    ins.then_inc(stats_step, 1)
                if s.within(NB):
                    n = rows_of(s)
                    wait(dve, xt_ready, s.n + 1)
                    wait(dve, xhi_ready, s.n + 1)

                    def part(t):
                        return t.rearrange("p (j r) -> p j r", j=J)[:, :, 0:n]
                    for k in range(2):
                        ins = v.tensor_tensor(part(xs_a[:, s.ring(2), 1, k]), part(psum[k][:]), part(xs_a[:, s.ring(2), 0, k]), ALU.subtract)
                    ins.then_inc(xlo_ready, 1)
                if stats:
                    wait(dve, stats_step, at + 1)
                    v.tensor_tensor(pq[:, 0], bn[:, :, 1], bn[:, :, 4], ALU.add)
                    v.tensor_tensor(pq[:, 1], bn[:, :, 1], bn[:, :, 4], ALU.subtract)
                    v.tensor_tensor(pq[:, 2], bn[:, :, 2], bn[:, :, 5], ALU.add).then_inc(stats_step, 1)
                t = s
                k, k4 = t.ring(2), t.ring(4)
                edges = t.within(NT)
                if edges:
                    wait(dve, dst_row, t.n + 1)
                    wait(dve, merged, (t - 1).n)
                    v.tensor_scalar(equal[:, k], psum[7][:, 0:P], dst_f[:, bass.ds(t.n, 1)], None, ALU.is_equal).then_inc(equal_ready, 1)
                if stats:
                    wait(dve, stats_step, at + 2)
                    v.scalar_tensor_tensor(pq[:, 3], pq[:, 1], 0.25, pq[:, 1], ALU.mult, ALU.mult).then_inc(stats_step, 1)
                if edges:
                    wait(dve, slots_in[k4], t.of(16, 4) + 16)
                    v.tensor_tensor(lead[:, k, 1:2], spare_row[:], slot_c[:, k4:k4 + 1], ALU.subtract).then_inc(lead_step, 1)
                    wait(dve, equal_ready, t.n + 1)
                    v.tensor_tensor_reduce(junk_p, equal[:, k], earlier[:], 1.0, 0.0, ALU.mult, ALU.add, lead[:, k, 0:1]).then_inc(lead_step, 1)
                if stats:
                    wait(dve, stats_step, at + 3)
                    v.scalar_tensor_tensor(pq[:, 4], pq[:, 2], 1.0 / C, pq[:, 3], ALU.mult, ALU.add).then_inc(stats_step, 1)
                if edges:
                    wait(dve, lead_step, 4 * t.n + 2)
                    v.tensor_scalar(lead[:, k, 2:3], lead[:, k, 0:1], 0.5, None, ALU.is_gt).then_inc(lead_step, 1)
                if stats:
                    wait(dve, stats_step, at + 4)
                    v.tensor_scalar(pow_in[:, kq, 0], pq[:, 4], LN_EPS, None, ALU.add).then_inc(stats_step, 1)
                if edges:
                    wait(dve, lead_step, 4 * t.n + 3)
                    wait(dve, added, (t - 3).of(16, 1))
                    v.scalar_tensor_tensor(goal[:, k4:k4 + 1], lead[:, k, 1:2], lead[:, k, 2:3], slot_c[:, k4:k4 + 1], ALU.mult, ALU.add).then_inc(lead_step, 1)
                if stats:
                    wait(dve, stats_step, at + 5)
                    v.reciprocal(pq[:, 5], pow_in[:, kq, 0]).then_inc(scale_step, 1)
                if edges:
                    wait(dve, filter_ready, t.n + 1)
                    wait(dve, emb_in[k4], t.of(16, 4) + 16)
                    v.scalar_tensor_tensor(msg[:, k], psum[5][:, 0:C], cut2[:, bass.ds(t.n, 1)], emb[:, k4], ALU.mult, ALU.mult).then_inc(msg_ready, 1)
                if stats:
                    wait(dve, scale_step, at + 1)
                    v.tensor_tensor(pq[:, 6], pq[:, 5], pq[:, 4], ALU.mult).then_inc(scale_step, 1)
                if stats:
                    wait(dve, scale_step, at + 2)
                    v.tensor_scalar(pow_in[:, kq, 1], pq[:, 6], RMS_FLOOR ** 2 / C, None, ALU.max).then_inc(pow_in_ready, 1)

            run_steps(dve, -3, NB + 2, *LOOP_A, step_a)

            dve.wait_ge(acc_step, NB)
            v.tensor_copy(small[:, 0:1], denom).then_inc(g_step, 1)
            dve.wait_ge(exp_ready, NB)
            dve.wait_ge(g_step, 1)
            v.tensor_copy(small[:, 1:2], small[:, 0:1]).then_inc(g_step, 1)
            dve.wait_ge(g_ps, 1)
            v.tensor_copy(acc_t, psum[0][:, 0:C].rearrange("p (k n) -> p k n", k=2))
            dve.wait_ge(g_ps, 2)
            v.tensor_copy(mem_t[0:MEM], psum[1][0:MEM, 0:2 * P].rearrange("p (k n) -> p k n", k=2)).then_inc(g_step, 1)
            dve.wait_ge(g_act, 1)
            v.tensor_tensor(small[:, 2:3], small[:, 0:1], small[:, 8:9], ALU.add).then_inc(g_step, 1)
            dve.wait_ge(g_step, 4)
            v.reciprocal(small[:, 3:4], small[:, 2:3]).then_inc(g_step, 1)
            dve.wait_ge(g_step, 5)
            v.tensor_scalar(small[:, 4:5], small[:, 3:4], float(DH) ** -0.5, None, ALU.mult).then_inc(g_step, 1)
            dve.wait_ge(g_ps, 3)
            v.tensor_tensor(ctx_t, psum[2][:, 0:P], same_head[:], ALU.mult).then_inc(g_step, 1)
            dve.wait_ge(g_step, 7)
            dve.wait_ge(g_ps, 4)
            v.tensor_scalar(g_f[:], psum[3][:, 0:C], small[:, 4:5], None, ALU.mult).then_inc(g_ready, 1)
            dve.wait_ge(added, 16 * NT)
            v.tensor_copy(small[:, 5:6], small[:, 4:5]).then_inc(stage_a_done, 1)

            def step_b(s):
                b = s + 2
                if b.within(NB):
                    k = b.ring(4)
                    wait(dve, s_ready, (b - 3).n)
                    v.tensor_copy(idx_b[:, k], agg_row[:, bass.ds(b.n * J, J)]).then_inc(idx_ready, 1)
                b = s - 2
                if b.within(NB):
                    n = rows_of(b)
                    wait(dve, comb_ready, b.n + 1)
                    wait(dve, s_ready, b.n + 1)
                    for h in range(2):
                        sv = slice(2 * h, 2 * h + 2)
                        ins = v.tensor_tensor(s_b[0:n, b.ring(4), sv], psum[4 + h][0:n, :].rearrange("p (j c) -> p j c", j=2), x_r[0:n, b.ring(4), sv], ALU.add)
                    ins.then_inc(u_ready, 1)
                b = s - 4
                if b.within(NB):
                    n = rows_of(b)
                    wait(dve, powb_ready, b.n + 1)
                    wait(dve, o_ready, (b - 3).n)
                    for j in range(J):
                        ins = v.scalar_tensor_tensor(x1[0:n, b.ring(4), j], psum[6 + j // 2][0:n, j % 2 * C:(j % 2 + 1) * C], powb_out[0:n, (b + 1).ring(2), 0, j:j + 1],
                                                     gout_r[0:n], ALU.mult, ALU.mult)
                    ins.then_inc(mix_used, 1)
                b = s - 6
                if b.within(NB):
                    cols = bass.ds(b.n * J, J)
                    mr, means, rr = mix_r[:, b.ring(4)], ln_b[:, b.ring(2), 0], powb_out[:, (b + 1).ring(2), 1]
                    wait(dve, powb_ready, b.n + 3)
                    v.tensor_scalar(mr[:, 2], rr, 1.0, None, ALU.add)
                    v.scalar_tensor_tensor(mr[:, 3], means, -0.5, rr, ALU.mult, ALU.mult).then_inc(factors_ready, 1)
                    v.tensor_copy(stat2[:, cols, 1], rr)
                if s.within(NB):
                    n = rows_of(s)
                    wait(dve, xbt_ready, s.n + 1)
                    wait(dve, bhi_ready, s.n + 1)

                    def part(t):
                        return t.rearrange("p (j r) -> p j r", j=J)[:, :, 0:n]
                    for k in range(2):
                        ins = v.tensor_tensor(part(xs_b[:, s.ring(2), 1, k]), part(psum[k][:]), part(xs_b[:, s.ring(2), 0, k]), ALU.subtract)
                    ins.then_inc(blo_ready, 1)
                b = s - 1
                if b.within(NB):
                    n, k = rows_of(b), b.ring(2)
                    wait(dve, q_ready, b.n + 1)
                    q4 = psum[2][0:n, :].rearrange("p (h d) -> p h d", d=DH)
                    v.tensor_reduce(q_max[0:n, k], q4, AX.X, ALU.max).then_inc(qmax_step, 1)
                    wait(dve, qmax_step, 2 * b.n + 1)
                    wait(dve, qt_ps, (b - 1).n)
                    v.tensor_tensor(q_e[0:n, k].rearrange("p (h d) -> p h d", d=DH), q4, q_max[0:n, k].unsqueeze(2).to_broadcast([n, 16, DH]), ALU.subtract).then_inc(qmax_step, 1)
                b = s - 4
                if b.within(NB):
                    n = rows_of(b)
                    wait(dve, mix_used, b.n + 1)
                    v.tensor_tensor(x1[0:n, b.ring(4)], x1[0:n, b.ring(4)], s_b[0:n, b.ring(4)], ALU.add).then_inc(x1_ready, 1)
                    wait(dve, x1_ready, b.n + 1)
                    moments(b, (0,))
                b = s - 1
                if b.within(NB):
                    n, k = rows_of(b), b.ring(2)
                    wait(dve, q_exp, b.n + 1)
                    v.tensor_reduce(q_sum[0:n, k], q_e[0:n, k].rearrange("p (h d) -> p h d", d=DH), AX.X, ALU.add).then_inc(q_sums, 1)
                    wait(dve, q_sums, 2 * b.n + 1)
                    v.reciprocal(q_inv[0:n, k], q_sum[0:n, k]).then_inc(q_sums, 1)
                b = s - 4
                if b.within(NB):
                    moments(b, (1,))
                b = s - 3
                if b.within(NB + 2):
                    if b.within(NB):
                        wait(dve, sumsq_ready, b.n + 1)
                    v.tensor_scalar(powb_in[:, s.ring(2), 0], sumsq[:, b.ring(4)], 1.0 / C, RMS_FLOOR ** 2 / C, ALU.mult, ALU.max).then_inc(powb_in_ready, 1)
                b = s - 4
                if b.within(NB):
                    lb_, cols, at = ln_b[:, b.ring(2)], bass.ds(b.n * J, J), b.of(4, 1)
                    moments(b, (2, 3)).then_inc(ln_step, 1)
                    wait(dve, ln_step, at + 1)
                    v.tensor_tensor(lb_[:, 0], bn_b[:, :, 1], bn_b[:, :, 4], ALU.add)
                    v.tensor_tensor(lb_[:, 1], bn_b[:, :, 1], bn_b[:, :, 4], ALU.subtract)
                    v.tensor_tensor(lb_[:, 2], bn_b[:, :, 2], bn_b[:, :, 5], ALU.add).then_inc(ln_step, 1)
                    v.tensor_copy(dot2[:, cols], lb_[:, 6])
                    wait(dve, ln_step, at + 2)
                    v.scalar_tensor_tensor(lb_[:, 3], lb_[:, 1], 0.25, lb_[:, 1], ALU.mult, ALU.mult)
                    v.tensor_scalar(lb_[:, 4], lb_[:, 2], 1.0 / C, LN_EPS, ALU.mult, ALU.add).then_inc(ln_step, 1)
                    v.tensor_scalar(stat2[:, cols, 0], lb_[:, 0], 0.5, None, ALU.mult)
                    wait(dve, ln_step, at + 3)
                    v.tensor_tensor(powb_in[:, (s + 1).ring(2), 1], lb_[:, 4], lb_[:, 3], ALU.add).then_inc(ln_step, 1)

            def moments(b, js):
                n = rows_of(b)
                for j in js:
                    v.bn_stats(bn_b[0:n, j], x1[0:n, b.ring(4), j])
                    ins = v.tensor_tensor_reduce(dot_junk[0:n, j], x1[0:n, b.ring(4), j], wr_r[0:n], 1.0, 0.0, ALU.mult, ALU.add, ln_b[0:n, b.ring(2), 6, j:j + 1])
                return ins

            v.memset(bn_b, 0.0)
            v.memset(ln_b, 0.0)
            chain(v.memset(mix_r, 1.0))
            run_steps(dve, -2, LAST_B, *LOOP_B, step_b)

            dve.wait_ge(factors_ready, NB)
            for k in range(2):
                dve.wait_ge(o_stored[k], 16 * (NB // 2))
            mean, r = stat2[:, :, 0], stat2[:, :, 1]
            chain(v.tensor_scalar(t_cmp, mean, wr_sum[:, 0:1], None, ALU.mult))
            chain(v.tensor_tensor(t_cmp, dot2[:], t_cmp, ALU.subtract))
            chain(v.tensor_tensor(t_cmp, t_cmp, r, ALU.mult))
            chain(v.tensor_scalar(stat2[:, :, 2], t_cmp, br_c[:, 0:1], None, ALU.add))
            chain(v.memset(w_all, LOWEST))
            chain(v.tensor_copy(w_all[:, 0:COLS - J], stat2[:, 0:COLS - J, 2]))
            chain(v.tensor_copy(w_all[0:TAIL, COLS - J:COLS], stat2[0:TAIL, COLS - J:COLS, 2]))
            chain(v.tensor_scalar(t_rank, r, 1.0, None, ALU.add))
            chain(v.reciprocal(t_gt, t_rank))
            chain(v.tensor_tensor(t_rank, r, t_gt, ALU.mult))
            v.tensor_copy(stat2[:, :, 1], t_rank).then_inc(params_ready, 1)

            key, bit, mask, cand, fl, take, sgn = (small_i[:, k:k + 1] for k in range(7))
            cnt = small[:, 16:17]
            v.tensor_scalar(t_cmp, w_all, 0.0, None, ALU.is_ge, ALU.add, accum_out=cnt).then_inc(t_counts, 1)
            dve.wait_ge(t_total, 1)
            chain(v.tensor_scalar(sgn, psum[0][:, 0:1], K_SEL - 0.5, None, ALU.is_lt))
            chain(v.tensor_scalar(key, sgn, 31, None, ALU.logical_shift_left))
            chain(v.tensor_scalar(mask, sgn, 31, 31, ALU.logical_shift_left, ALU.arith_shift_right))
            chain(v.tensor_scalar(mask, mask, 0x7FFFFFFF, None, ALU.bitwise_and))
            chain(v.memset(take, 1))
            chain(v.tensor_scalar(bit, take, 30, None, ALU.logical_shift_left))
            with dve.Fori(0, 31) as i:
                v.tensor_tensor(cand, key, bit, ALU.bitwise_or).then_inc(t_step, 1)
                wait(dve, t_step, i * 5 + 1)
                v.tensor_tensor(fl, cand, mask, ALU.bitwise_xor).then_inc(t_step, 1)
                wait(dve, t_step, i * 5 + 2)
                v.tensor_scalar(t_cmp, w_all, fl.bitcast(F32), None, ALU.is_lt, ALU.add, accum_out=cnt).then_inc(t_counts, 1)
                wait(dve, t_total, i + 2)
                v.scalar_tensor_tensor(take, psum[0][:, 0:1], P * COLS - K_SEL + 0.5, bit, ALU.is_lt, ALU.mult).then_inc(t_step, 1)
                wait(dve, t_step, i * 5 + 3)
                v.tensor_tensor(key, key, take, ALU.bitwise_or).then_inc(t_step, 1)
                v.tensor_scalar(bit, bit, 1, None, ALU.logical_shift_right).then_inc(t_step, 1)
                wait(dve, t_step, i * 5 + 5)
            chain(v.tensor_tensor(fl, key, mask, ALU.bitwise_xor))
            chain(v.tensor_scalar(t_eq, w_all, fl.bitcast(F32), None, ALU.is_equal))
            v.tensor_scalar(t_gt, w_all, fl.bitcast(F32), None, ALU.is_gt, ALU.add, accum_out=cnt).then_inc(t_counts, 1)
            dve.wait_ge(t_total, 33)
            chain(v.tensor_scalar(small[:, 18:19], psum[0][:, 0:1], -1.0, float(K_SEL), ALU.mult, ALU.add))
            ranks(t_eq, t_rank, t_rk, 2)
            chain(v.tensor_scalar(t_cmp, t_rank, small[:, 18:19], None, ALU.is_lt))
            chain(v.tensor_tensor(t_cmp, t_cmp, t_eq, ALU.mult))
            chain(v.tensor_tensor(t_sel, t_cmp, t_gt, ALU.add))
            ranks(t_sel, t_rank, t_rk, 3)
            chain(v.tensor_copy(t_ri[:, 0], t_rank))
            chain(v.tensor_scalar(t_ri[:, 1], t_ri[:, 0], 127, None, ALU.bitwise_and))
            chain(v.tensor_scalar(t_ri[:, 2], t_ri[:, 0], 7, None, ALU.logical_shift_right))
            chain(v.tensor_copy(t_lane, t_ri[:, 1]))
            chain(v.tensor_copy(t_fi, t_rk[:, 2]))
            chain(v.tensor_scalar(t_fi, t_fi, 7, None, ALU.logical_shift_right))
            chain(v.tensor_copy(t_first, t_fi))
            chain(v.tensor_copy(t_rel, t_ri[:, 2]))
            r3 = t_rel.rearrange("p (b j) -> p b j", j=J)
            chain(v.tensor_tensor(r3, r3, t_first.unsqueeze(2).to_broadcast([P, NB, J]), ALU.subtract))
            chain(v.tensor_scalar(t_rel, t_rel, 1.0, None, ALU.add))
            chain(v.tensor_tensor(t_rel, t_rel, t_sel, ALU.mult))
            chain(v.tensor_scalar(t_rel, t_rel, 1.0, None, ALU.subtract))
            chain(v.tensor_copy(iota_b, iota_c[:, 0:P]))
            chain(v.tensor_copy(t_ri[:, 0], iota_c[:, 0:COLS]))
            chain(v.tensor_scalar(t_ri[:, 0], t_ri[:, 0], J - 1, None, ALU.bitwise_and))
            chain(v.tensor_copy(j_pat, t_ri[:, 0]))
            chain(v.tensor_tensor(hot5[:, :, 0], t_rel.unsqueeze(2).to_broadcast([P, COLS, REL]), iota_c[:, 0:REL].unsqueeze(1).to_broadcast([P, COLS, REL]), ALU.is_equal))
            chain(v.tensor_scalar(hot5[:, :, 1], hot5[:, :, 0], lane_id[:, 0:1], None, ALU.mult))
            chain(v.tensor_tensor(hot5[:, :, 2], hot5[:, :, 0], j_pat.unsqueeze(2).to_broadcast([P, COLS, REL]), ALU.mult))

            for b in range(NB):
                if b >= 4:
                    dve.wait_ge(hotl_used, b - 3)
                v.tensor_tensor(hot_l[:, b % 4], t_lane[:, b * J:(b + 1) * J].unsqueeze(2).to_broadcast([P, J, P]),
                                iota_b.unsqueeze(1).to_broadcast([P, J, P]), ALU.is_equal).then_inc(hotl_ready, 1)
            dve.wait_ge(hotl_used, NB)
            chain(v.tensor_scalar(blk512, iota_c[:, 0:NB], float(BLOCK), None, ALU.mult))
            PER = 512 // (3 * REL)
            for q in range(-(-NB // PER)):
                n = min(PER, NB - q * PER)
                pp = psum[1 + q][:, 0:n * 3 * REL].rearrange("p (b k r) -> p k r b", k=3, r=REL)
                p1, p2 = part[:, :, q * PER:q * PER + n], part2[:, :, q * PER:q * PER + n]
                bb = blk512[:, q * PER:q * PER + n].unsqueeze(1).to_broadcast([P, REL, n])
                chain(v.tensor_tensor(p1, pp[:, 0], bb, ALU.mult))
                chain(v.tensor_scalar(p2, pp[:, 1], float(J), None, ALU.mult))
                chain(v.tensor_tensor(p1, p1, p2, ALU.add))
                chain(v.tensor_tensor(p1, p1, pp[:, 2], ALU.add))
            v.tensor_copy(small[:, 20:21], small[:, 18:19]).then_inc(part_ready, 1)
            dve.wait_ge(part_tr, 1)
            chain(v.tensor_copy(part_t[0:NB, 0:4], psum[6][0:NB, 0:4 * P].rearrange("p (r n) -> p r n", n=P)))
            chain(v.tensor_copy(part_t[0:NB, 4], psum[7][0:NB, 0:P]))
            chain(v.tensor_copy(first_c[0:NB], psum[7][0:NB, P:P + 1]))
            for k in range(REL):
                chain(v.tensor_scalar(small[0:NB, 24 + k:25 + k], first_c[0:NB], float(k), None, ALU.add))
                chain(v.tensor_scalar(place[0:NB, k], iota_c[0:NB, 0:LISTED], small[0:NB, 24 + k:25 + k], None, ALU.is_equal))
            v.tensor_copy(small[:, 21:22], small[:, 20:21]).then_inc(part_in, 1)
            chain(v.tensor_scalar(pad_far, iota_c[:, 0:LISTED], float(P), lane_id[:, 0:1], ALU.mult, ALU.add))
            chain(v.tensor_scalar(pad_far, pad_far, K_SEL - 0.5, FAR, ALU.is_gt, ALU.mult))
            dve.wait_ge(list_ps, 1)
            chain(v.tensor_tensor(list_keep[:], psum[5][:, 0:LISTED], pad_far, ALU.add))

            chain(v.memset(g_r, 0.0))
            chain(v.memset(par, 0.0))

            def step_c(s):
                b = s + 1
                if s.within(NC):
                    k = s.ring(2)
                    wait(dve, y_ps, (s - 1).of(2, 1))
                    for m in range(FK):
                        wait(dve, h_act, s.of(FK, 1) + m + 1)
                        v.tensor_copy(h_s[:, k, 0, m], h_f[:, m % 4]).then_inc(h_hi, 1)
                        wait(dve, h_hi, s.of(FK, 1) + m + 1)
                        v.tensor_tensor(h_s[:, k, 1, m], h_f[:, m % 4], h_s[:, k, 0, m], ALU.subtract).then_inc(h_lo, 1)
                        if m == FK // 2 - 1 and b.within(NC):
                            normalise_c(b)
                        if m == FK - 3 and (s + 2).within(NC):
                            columns_c(s + 2)
                else:
                    if (s + 2).within(NC):
                        columns_c(s + 2)
                    if b.within(NC):
                        normalise_c(b)
                if b.within(NC):
                    wait(dve, ct_ready, b.n + 1)
                    wait(dve, chi_ready, b.n + 1)
                    for h in range(2):
                        ins = v.tensor_tensor(xs_c[:, b.ring(2), 1, h], psum[h][:], xs_c[:, b.ring(2), 0, h], ALU.subtract)
                    ins.then_inc(clo_ready, 1)
                b = s - 1
                if b.within(NC):
                    for h in range(2):
                        finish_c(b, h)

            def columns_c(b):
                k = b.ring(4)
                wait(dve, scattered[k], b.of(16 * J, 4))
                v.tensor_copy(row_c[:, k], list_keep[:, bass.ds(b.n * J, J)]).then_inc(cols_c, 1)

            def normalise_c(b):
                k4, k = b.ring(4), b.ring(2)
                wait(dve, rows_in[k4], b.of(16 * J, 4) + 16 * J)
                wait(dve, pars_in[k4], b.of(16 * J, 4) + 16 * J)
                wait(dve, ct_ready, (b - 1).n)
                for j in range(J):
                    ins = v.tensor_scalar(ln_c[:, k, j], g_r[:, k4, j], par[:, k4, j, 0:1], par[:, k4, j, 1:2], ALU.subtract, ALU.mult)
                ins.then_inc(ln_ready, 1)

            def finish_c(b, h):
                k4 = b.ring(4)
                wait(dve, y_ps, b.of(2, 1) + h + 1)
                for j in (2 * h, 2 * h + 1):
                    row = g_r[:, k4, j]
                    ins = v.scalar_tensor_tensor(row, psum[6 + h][:, j % 2 * C:(j % 2 + 1) * C], par[:, k4, j, 2:3], row, ALU.mult, ALU.add)
                ins.then_inc(y_ready if h else y_half, 1)

            run_steps(dve, -2, NC, *LOOP_C, step_c)

        @block.tensor
        def _(pe):
            t_ = nc.tensor

            def mm(o, lhs, rhs, first, last):
                return t_.matmul(o, lhs, rhs, start=first, stop=last)

            def three(o, lhs, rhs, more=(), open_=True, close=True):
                n = 0
                todo = [(x, y, k) for k in range(2) for x, y in HI_LO]
                for x, y, k in todo:
                    ins = mm(o, lhs(x, k), rhs(y, k), open_ and n == 0, close and n == len(todo) - 1)
                    n += 1
                return ins

            def rank_totals(mask_sums, turn):
                pe.wait_ge(rank_in, turn)
                mm(psum[4][:, 0:NB], before[:], mask_sums, True, True)
                mm(psum[5][:, 0:NB], ones[:], mask_sums, True, True).then_inc(rank_sums, 1)

            pe.wait_ge(constants_ready, 3)

            def count_tile(k, ready, first, last):
                wait(pe, hot_ready, ready)
                ins = mm(psum[7][:, 0:COLS], hot_p[:, k], hot_c[:, k], first, last)
                ins.then_inc(counted if last else hot_used, 1)

            count_tile(0, 1, True, False)
            count_tile(1, 2, False, False)
            with pe.Fori(0, NT // 2 - 2) as i:
                for k in range(2):
                    count_tile(k, i * 2 + (3 + k), False, False)
            count_tile(0, NT - 1, False, False)
            count_tile(1, NT, False, True)
            rank_totals(rk[:, 0], 1)
            pe.wait_ge(weights_ready, 1)

            def step_a(s):
                b = s - 2
                if b.within(NB):
                    n = rows_of(b)
                    wait(pe, exp_ready, b.n + 1)
                    wait(pe, en_ready, (b).n)
                    for j in range(J):
                        ins = t_.transpose(psum[3][0:n, j * P:(j + 1) * P], e_t[:, b.ring(2), j * n:(j + 1) * n], ident[:])
                    ins.then_inc(et_ready, 1)
                b = s - 1
                if b.within(NB):
                    n = rows_of(b)
                    wait(pe, xhi_ready, b.n + 1)
                    wait(pe, xlo_ready, b.n + 1)
                    wait(pe, exp_ready, b.n)
                    three(psum[2][:, 0:n * J], lambda x, k: wk_s[:, x, k],
                          lambda y, k: xs_a[:, b.ring(2), y, k].rearrange("p (j r) -> p j r", j=J)[:, :, 0:n]).then_inc(keys_ready, 1)
                if s.within(NB):
                    n = rows_of(s)
                    wait(pe, normed, s.n + 1)
                    wait(pe, xlo_ready, s.n)
                    for k in range(2):
                        for j in range(J):
                            ins = t_.transpose(psum[k][:, j * P:j * P + n], xr[0:n, s.ring(4), j, k * P:(k + 1) * P], ident[0:n, 0:n])
                    ins.then_inc(xt_ready, 1)
                t = s
                if t.within(NT):
                    k = t.ring(2)
                    wait(pe, edge_cols, t.n + 1)
                    wait(pe, msg_ready, t.n)
                    t_.transpose(psum[5][:, 0:P], attr_c[:, k], ident[:]).then_inc(attr_tr, 1)
                    mm(psum[7][:, 0:P], ones[:], diag[:, k], True, True).then_inc(dst_row, 1)
                if t.within(NT):
                    wait(pe, attr_t_ready, t.n + 1)
                    mm(psum[5][:, 0:C], attr_t[0:RBF + 1, k], wd_f[:], True, True).then_inc(filter_ready, 1)
                t = s - 1
                if t.within(NT):
                    k = t.ring(2)
                    wait(pe, msg_ready, t.n + 1)
                    wait(pe, contrib_ready, t.n)
                    for h in range(2):
                        ins = mm(psum[6][:, h * P:(h + 1) * P], msg[:, k, h * P:(h + 1) * P], equal[:, k], True, True)
                    ins.then_inc(merged, 1)
                b = s - 2
                if b.within(NB):
                    n = rows_of(b)
                    wait(pe, en_ready, b.n + 1)
                    wait(pe, acc_step, b.n)
                    for j in range(J):
                        ins = mm(psum[4][:, 0:C], e_n[0:n, b.ring(2), j * P:(j + 1) * P], xr[0:n, b.ring(4), j], j == 0, j == J - 1)
                    ins.then_inc(sums_ready, 1)
                t = s - 1
                if t.within(NT):
                    k = t.ring(2)
                    wait(pe, merged_t, t.n + 1)
                    for h in range(2):
                        ins = mm(psum[6][:, C:2 * C], msg_t[:, k, h * P:(h + 1) * P], wb_f[:, h], h == 0, h == 1)
                    ins.then_inc(contrib_ps, 1)

            run_steps(pe, 0, NB + 1, *LOOP_A, step_a)

            pe.wait_ge(acc_step, NB)
            pe.wait_ge(xlo_ready, NB)
            pe.wait_ge(exp_ready, NB)
            pe.wait_ge(g_act, 1)
            for k in range(2):
                ins = t_.transpose(psum[0][:, k * P:(k + 1) * P], acc[:, k * P:(k + 1) * P], ident[:])
            ins.then_inc(g_ps, 1)
            t_.transpose(psum[1][0:MEM, 0:P], mem_e, ident[:])
            t_.transpose(psum[1][0:MEM, P:2 * P], mem_v[:], ident[:]).then_inc(g_ps, 1)
            pe.wait_ge(g_step, 3)
            for k in range(2):
                mm(psum[2][:, 0:P], wv_f[:, k], acc_t[:, k], k == 0, False)
            mm(psum[2][:, 0:P], mem_t[0:MEM, 1], mem_t[0:MEM, 0], False, True).then_inc(g_ps, 1)
            pe.wait_ge(g_step, 7)
            pe.wait_ge(en_ready, NB)
            mm(psum[3][:, 0:C], ctx_t, wo_f[:], True, True).then_inc(g_ps, 1)
            pe.wait_ge(stage_a_done, 1)

            def step_b(s):
                if s.within(NB):
                    n = rows_of(s)
                    wait(pe, xn_ready, s.n + 1)
                    wait(pe, blo_ready, s.n)
                    for k in range(2):
                        for j in range(J):
                            ins = t_.transpose(psum[k][:, j * P:j * P + n], xn[0:n, s.ring(2), j, k * P:(k + 1) * P], ident[0:n, 0:n])
                    ins.then_inc(xbt_ready, 1)
                b = s - 1
                if b.within(NB):
                    n, kk = rows_of(b), b.ring(2)
                    wait(pe, bhi_ready, b.n + 1)
                    wait(pe, blo_ready, b.n + 1)
                    wait(pe, qmax_step, b.of(2, 1))
                    for j in range(J):
                        ins = three(psum[2][0:n, j * P:(j + 1) * P], lambda x, k: xs_b[:, kk, x, k, j * P:j * P + n], lambda y, k: wq_s[:, y, k])
                    ins.then_inc(q_ready, 1)
                b = s - 3
                if b.within(NB):
                    n = rows_of(b)
                    wait(pe, qt_ready, b.n + 1)
                    wait(pe, mix_used, b.n)
                    for j in range(J):
                        o = psum[6 + j // 2][0:n, j % 2 * C:(j % 2 + 1) * C]
                        mm(o, q_t[:, b.ring(2), j * P:j * P + n], g_f[:], True, False)
                        ins = mm(o, ones_b[:, 0:n], bias_b[:, 1], False, True)
                    ins.then_inc(mix_ready, 1)
                b = s - 1
                if b.within(NB):
                    n, kk = rows_of(b), b.ring(2)
                    wait(pe, u_ready, b.n)
                    for j in range(J):
                        o = psum[4 + j // 2][0:n, j % 2 * C:(j % 2 + 1) * C]
                        three(o, lambda x, k: xs_b[:, kk, x, k, j * P:j * P + n], lambda y, k: wc_s[:, y, k], close=False)
                        ins = mm(o, ones_b[:, 0:n], bias_b[:, 0], False, True)
                    ins.then_inc(comb_ready, 1)
                b = s - 2
                if b.within(NB):
                    n = rows_of(b)
                    wait(pe, q_scaled, b.n + 1)
                    wait(pe, qt_ready, b.n)
                    for j in range(J):
                        ins = t_.transpose(psum[3][:, j * P:j * P + n], q_e[0:n, b.ring(2), j * P:(j + 1) * P], ident[0:n, 0:n])
                    ins.then_inc(qt_ps, 1)

            run_steps(pe, 0, NB + 2, *LOOP_B, step_b)

            pe.wait_ge(t_counts, 1)
            mm(psum[0][:, 0:1], ones[:], small[:, 16:17], True, True).then_inc(t_total, 1)
            with pe.Fori(0, 31) as i:
                wait(pe, t_counts, i + 2)
                mm(psum[0][:, 0:1], ones[:], small[:, 16:17], True, True).then_inc(t_total, 1)
            pe.wait_ge(t_counts, 33)
            mm(psum[0][:, 0:1], ones[:], small[:, 16:17], True, True).then_inc(t_total, 1)
            rank_totals(t_rk[:, 0], 2)
            rank_totals(t_rk[:, 0], 3)
            PER = 512 // (3 * REL)
            for b in range(NB):
                pe.wait_ge(hotl_ready, b + 1)
                q, at = b // PER, b % PER * 3 * REL
                for j in range(J):
                    ins = mm(psum[1 + q][:, at:at + 3 * REL], hot_l[:, b % 4, j], hot5[:, b * J + j].rearrange("p k r -> p (k r)"), j == 0, j == J - 1)
                ins.then_inc(hotl_used, 1)
            pe.wait_ge(part_ready, 1)
            for k in range(4):
                t_.transpose(psum[6][0:NB, k * P:(k + 1) * P], part[:, k], ident[:])
            t_.transpose(psum[7][0:NB, 0:P], part[:, 4], ident[:])
            t_.transpose(psum[7][0:NB, P:2 * P], t_first, ident[:]).then_inc(part_tr, 1)
            pe.wait_ge(part_in, 1)
            for k in range(REL):
                ins = mm(psum[5][:, 0:LISTED], part_t[0:NB, k], place[0:NB, k], k == 0, k == REL - 1)
            ins.then_inc(list_ps, 1)

            def step_c(s):
                if s.within(NC):
                    kk = s.ring(2)
                    wait(pe, chi_ready, s.n + 1)
                    wait(pe, clo_ready, s.n + 1)
                    for m in range(FK):
                        wait(pe, h_act, s.of(FK, 1) + m - 3)
                        three(psum[2 + m % 4][:], lambda x, k: w1_s[:, x, k, m * P:(m + 1) * P], lambda y, k: xs_c[:, kk, y, k]).then_inc(h_ps, 1)
                b = s + 1
                if b.within(NC):
                    wait(pe, ln_ready, b.n + 1)
                    wait(pe, clo_ready, b.n)
                    for k in range(2):
                        for j in range(J):
                            ins = t_.transpose(psum[k][:, j * P:(j + 1) * P], ln_c[:, b.ring(2), j, k * P:(k + 1) * P], ident[:])
                    ins.then_inc(ct_ready, 1)
                b = s - 1
                if b.within(NC):
                    kk = b.ring(2)
                    wait(pe, h_lo, b.of(FK, 1) + FK)
                    for h in range(2):
                        wait(pe, y_half if h == 0 else y_ready, b.n)
                        for j in (2 * h, 2 * h + 1):
                            o = psum[6 + h][:, j % 2 * C:(j % 2 + 1) * C]
                            for m in range(FK):
                                for x, y in HI_LO:
                                    mm(o, h_s[:, kk, x, m, j * P:(j + 1) * P], w2_s[:, y, m], m == 0 and (x, y) == (0, 0), False)
                            ins = mm(o, ones_b[:], bias_b[:, 2], False, True)
                        ins.then_inc(y_ps, 1)

            run_steps(pe, -1, NC, *LOOP_C, step_c)


NAMES = ["x", "src", "dst", "edge_attr_64", "edge_weight", "node_type_100", "L0_gnn_embed_table", "L0_gnn_W_dist", "L0_gnn_b_dist", "L0_gnn_W_comb",
         "L0_gnn_b_comb", "L0_mix_w_qkv", "L0_mix_mem_kv", "L0_mix_w_out", "L0_mix_b_out", "L0_mix_g_out", "L0_mix_g_pre", "L0_ffn_wr", "L0_ffn_br",
         "L0_ffn_w1", "L0_ffn_b1", "L0_ffn_w2", "L0_ffn_b2"]


def kernel(**inputs):
    import concourse.bacc as bacc
    from concourse.bass_utils import run_bass_kernel_spmd

    nc = bacc.Bacc("TRN2", target_bir_lowering=False, num_devices=1)
    arrays, args = {}, {}
    for name in NAMES:
        v = np.ascontiguousarray(inputs[name])
        arrays[f"in_{name}"] = v
        args[name] = nc.dram_tensor(f"in_{name}", v.shape, mybir.dt.from_np(v.dtype), kind="ExternalInput").ap()
    out = nc.dram_tensor("layer_out", inputs["x"].shape, F32, kind="ExternalOutput").ap()
    graph_layer(nc, args, out)
    return run_bass_kernel_spmd(nc, [arrays], core_ids=[0]).results[0]["layer_out"]
```

```python
from contextlib import ExitStack

import numpy as np

import concourse.bass as bass
from concourse import mybir

F32 = mybir.dt.float32
BF16 = mybir.dt.bfloat16
F16 = mybir.dt.float16
I32 = mybir.dt.int32
ALU = mybir.AluOpType
ACT = mybir.ActivationFunctionType
AX = mybir.AxisListType

P = 128
J = 4
BLOCK = P * J
LN_EPS = 1e-5
RMS_FLOOR = 1e-12
CUTOFF = 5.0
FAR = float(1 << 20)
LOWEST = -3.0e38


class Step:

    def __init__(self, i, base):
        self.i, self.base = i, base

    def __add__(self, k):
        return Step(self.i, self.base + k)

    def __sub__(self, k):
        return Step(self.i, self.base - k)

    def of(self, scale, per):
        here = self.base // per * scale
        return here if self.i is None else self.i * (4 // per * scale) + here

    @property
    def n(self):
        return self.of(1, 1)

    def ring(self, k):
        return self.base % k

    def within(self, count):
        return self.i is not None or 0 <= self.base < count

    def is_last(self, count):
        return self.i is None and self.base == count - 1


def run_steps(eng, first, last, loop_from, loop_to, body):
    for n in range(first, loop_from):
        body(Step(None, n))
    with eng.Fori(0, (loop_to - loop_from) // 4) as i:
        for v in range(4):
            body(Step(i, loop_from + v))
    for n in range(loop_to, last + 1):
        body(Step(None, n))


def graph_layer(nc, a, out):
    x_d = a["x"]
    N, C = x_d.shape
    E = a["src"].shape[0]
    RBF = a["edge_attr_64"].shape[1]
    HID = a["L0_mix_w_out"].shape[0]
    HEADS = a["L0_mix_mem_kv"].shape[1]
    DH = HID // HEADS
    MEM = a["L0_mix_mem_kv"].shape[3]
    SPECIES = a["L0_gnn_embed_table"].shape[0]
    FF = a["L0_ffn_w1"].shape[1]
    NB = -(-N // BLOCK)
    COLS = NB * J
    TAIL = (N - (NB - 1) * BLOCK) // J
    NT = -(-E // P)
    assert C == 2 * P and HID == P and N % J == 0 and 0 < TAIL < P and NT == NB and NB % 2 == 0
    FULL_LANES, LAST_LANE = E // NT, E % NT
    K_SEL = N // 2 - 1
    NC = -(-K_SEL // BLOCK)
    LISTED = NC * J
    SLOTS = E + 1
    TABLE = -(-(SLOTS + P) // P) * P
    FK = FF // P
    REL = J + 1
    PER = 512 // (3 * REL) // 4 * 4
    HI_LO = ((0, 0), (1, 0), (0, 1))

    ctx = ExitStack()
    with ctx:
        def sb(name, shape, dt=F32):
            return ctx.enter_context(nc.sbuf_tensor(name, shape, dt))

        def sem(name):
            return ctx.enter_context(nc.semaphore(name))

        ident = sb("ident", [P, P])
        ones = sb("ones", [P, P])
        ones_b = sb("ones_b", [P, P], BF16)
        bias_tmp = sb("bias_tmp", [P, 2, C], BF16)
        before = sb("before", [P, P])
        earlier = sb("earlier", [P, P])
        same_head = sb("same_head", [P, P])
        iota_c = sb("iota_c", [P, max(COLS, LISTED, P)])
        iota_h = sb("iota_h", [P, max(COLS, P)], F16)
        lane_id = sb("lane_id", [P, 1])
        spare_row = sb("spare_row", [P, 1])
        half_neg = sb("half_neg", [P, 16])
        wk_s = sb("wk_s", [P, 2, 2, P], BF16)
        wq_s = sb("wq_s", [P, 2, 2, P], BF16)
        wc_s = sb("wc_s", [P, 2, 2, C], BF16)
        w1_s = sb("w1_s", [P, 2, 2, FF], BF16)
        w2_s = sb("w2_s", [P, 2, FK, C], BF16)
        wv_f = sb("wv_f", [P, 2, P])
        wb_f = sb("wb_f", [P, 2, C])
        wd_f = sb("wd_f", [RBF + 1, C])
        wo_f = sb("wo_f", [P, C])
        bias_b = sb("bias_b", [P, 2, C], BF16)
        b1_c = sb("b1_c", [P, FK])
        gout_r = sb("gout_r", [P, C])
        b2_r = sb("b2_r", [P, C])
        wr_r = sb("wr_r", [P, C])
        br_c = sb("br_c", [P, 1])
        wr_sum = sb("wr_sum", [P, 1])
        mem_k = sb("mem_k", [P, MEM])
        mem_v = sb("mem_v", [P, MEM])
        g_f = sb("g_f", [P, C])
        inv_sd = sb("inv_sd", [P, COLS])
        inv_rms = sb("inv_rms", [P, COLS])
        shift = sb("shift", [P, COLS])
        agg_row = sb("agg_row", [P, COLS], I32)
        stat2 = sb("stat2", [P, COLS, 4])
        dot2 = sb("dot2", [P, COLS])
        small = sb("small", [P, 64])
        small_i = sb("small_i", [P, 20], I32)

        AREA = 35000
        area = sb("area", [P, AREA])

        class Layout:
            def __init__(self):
                self.at = 0

            def __call__(self, *dims, dt=F32):
                size = int(np.prod(dims))
                words = size // 2 if dt in (BF16, F16) else size
                v = area[:, self.at:self.at + words]
                self.at += words
                assert self.at <= AREA, self.at
                if dt != F32:
                    v = v.bitcast(dt)
                names = " ".join(f"d{k}" for k in range(len(dims)))
                kw = {f"d{k}": dims[k] for k in range(len(dims))}
                return v.rearrange(f"p ({names}) -> p {names}", **kw) if len(dims) > 1 else v

        la = Layout()
        x_r = la(4, J, C)
        xr = la(4, J, C)
        xs_a = la(2, 2, 2, BLOCK, dt=BF16)
        e_t = la(2, BLOCK)
        e_n = la(2, BLOCK)
        bn = la(8, 6)
        pair = la(2, 12, 8)
        pow_in = la(2, 2, 8)
        pow_out = la(2, 2, 8)
        run_max = la(4)
        neg_max = la(4)
        blk_max = la(4)
        decay = la(4)
        row_sum = la(4)
        denom = la(1)
        acc = la(C)
        attr = la(NT, RBF)
        ends = la(2, NT, dt=I32)
        dst_f = la(NT)
        dst_p = la(NT)
        dst_c = la(NT)
        ei = la(3, NT, dt=I32)
        cut = la(NT)
        cut2 = la(NT)
        hot_p = la(4, P, dt=BF16)
        hot_c = la(4, COLS, dt=BF16)
        zero = la(C)
        count = la(COLS)
        touched = la(COLS)
        rank = la(COLS)
        rk = la(3, NB)
        slot_i = la(COLS, dt=I32)
        end_c = la(4, 2, dt=I32)
        kind_c = la(4, dt=I32)
        slot_c = la(4, dt=I32)
        goal = la(4, dt=I32)
        emb = la(4, C)
        attr_c = la(2, P)
        attr_t = la(2, P)
        diag = la(2, P)
        equal = la(2, P)
        junk_p = la(P)
        lead = la(2, 4)
        msg = la(2, C)
        msg_t = la(2, C)
        contrib = la(2, C)
        st_qkv = la(2, 3 * P)
        st_comb = la(2, C)
        g_pre = la(2)
        st_bias = la(2, C)
        sp_bias = la(2, 2, C)
        acc_t = la(2, P)
        mem_e = la(MEM)
        mem_t = la(2, P)
        ctx_t = la(P)

        lb = Layout()
        lb(4, J, C)
        xn = lb(2, J, C)
        s_b = lb(4, J, C)
        ag = lb(2, J, C)
        xs_b = lb(2, 2, 2, BLOCK, dt=BF16)
        q_e = lb(2, BLOCK)
        q_t = lb(2, BLOCK)
        q_max = lb(2, 16)
        q_sum = lb(2, 16)
        q_inv = lb(2, 16)
        sq_junk = lb(J, C)
        dot_junk = lb(J, C)
        sumsq = lb(4, J)
        mix_r = lb(4, 4, J)
        x1 = lb(4, J, C)
        o_b = lb(2, J, C)
        var_junk = lb(2, J, C)
        varsum = lb(4, J)
        ln_b = lb(2, 8, J)
        powb_in = lb(2, 2, J)
        powb_out = lb(2, 2, J)
        idx_b = lb(4, J, dt=I32)

        lt = Layout()
        w_all = lt(COLS)
        t_cmp = lt(COLS)
        t_cmp3 = lt(3, COLS)
        t_gt = lt(COLS)
        t_eq = lt(COLS)
        t_sel = lt(COLS)
        t_rank = lt(COLS)
        t_rk = lt(3, NB)
        t_ri = lt(3, COLS, dt=I32)
        t_lane = lt(COLS, dt=F16)
        t_rel = lt(COLS)
        t_first = lt(NB)
        t_fi = lt(NB, dt=I32)
        j_pat = lt(COLS)
        hot5 = lt(COLS, 3, REL, dt=BF16)
        hot_l = lt(4, 2 * J, P, dt=BF16)
        part = lt(REL, NB)
        part2 = lt(REL, NB)
        blk512 = lt(NB)
        part_t = lt(REL, P)
        first_c = lt(1)
        place = lt(REL, LISTED)
        pad_far = lt(LISTED)
        st_w1 = lt(2, FF)
        st_w2 = lt(FK, C)

        lc = Layout()
        row_c = lc(4, J, dt=I32)
        g_r = lc(4, J, C)
        par = lc(4, J, 4)
        ln_c = lc(2, J, C)
        xs_c = lc(2, 2, 2, BLOCK, dt=BF16)
        h_f = lc(4, BLOCK)
        h_s = lc(2, 2, FK, BLOCK, dt=BF16)
        list_keep = sb("list_keep", [P, LISTED], I32)

        slot_tab = nc.dram_tensor("slot_tab", [NB * BLOCK, 1], I32, kind="Internal").ap()
        agg_tab = nc.dram_tensor("agg_tab", [TABLE, C], F32, kind="Internal").ap()
        row_tab = nc.dram_tensor("row_tab", [NB * BLOCK, 4], F32, kind="Internal").ap()

        psum = [ctx.enter_context(nc.psum_tensor(f"bank{k}", [P, 512], F32)) for k in range(8)]

        constants_ready = sem("constants_ready")
        pool_init = sem("pool_init")
        dve_init = sem("dve_init")
        weights_in = sem("weights_in")
        edges_in = sem("edges_in")
        table_zeroed = sem("table_zeroed")
        weights_ready = sem("weights_ready")
        ffn_in = sem("ffn_in")
        ffn_upper = sem("ffn_upper")
        ffn_ready = sem("ffn_ready")
        bias_act = sem("bias_act")
        bias_pool = sem("bias_pool")
        qkv_scaled = sem("qkv_scaled")
        comb_plus = sem("comb_plus")
        halves_ready = sem("halves_ready")
        angle_ready = sem("angle_ready")
        cos_ready = sem("cos_ready")
        hot_ready = sem("hot_ready")
        hot_used = sem("hot_used")
        counted = sem("counted")
        rank_in = sem("rank_in")
        rank_sums = sem("rank_sums")
        rank_step = sem("rank_step")
        slots_ready = sem("slots_ready")
        slots_stored = sem("slots_stored")
        x_in = [sem(f"x_in{k}") for k in range(4)]
        stats_step = sem("stats_step")
        pow_in_ready = sem("pow_in_ready")
        pow_ready = sem("pow_ready")
        scale_step = sem("scale_step")
        normed = sem("normed")
        xt_ready = sem("xt_ready")
        xhi_ready = sem("xhi_ready")
        xlo_ready = sem("xlo_ready")
        keys_ready = sem("keys_ready")
        max_step = sem("max_step")
        exp_ready = sem("exp_ready")
        et_ready = sem("et_ready")
        en_ready = sem("en_ready")
        sums_ready = sem("sums_ready")
        acc_step = sem("acc_step")
        ends_ready = sem("ends_ready")
        kinds_in = [sem(f"kinds_in{k}") for k in range(4)]
        slots_in = [sem(f"slots_in{k}") for k in range(4)]
        emb_in = [sem(f"emb_in{k}") for k in range(4)]
        edge_cols = sem("edge_cols")
        attr_tr = sem("attr_tr")
        attr_t_ready = sem("attr_t_ready")
        dst_row = sem("dst_row")
        filter_ready = sem("filter_ready")
        equal_ready = sem("equal_ready")
        lead_step = sem("lead_step")
        msg_ready = sem("msg_ready")
        merged = sem("merged")
        merged_t = sem("merged_t")
        contrib_ps = sem("contrib_ps")
        contrib_ready = sem("contrib_ready")
        added = sem("added")
        stage_a_done = sem("stage_a_done")
        g_step = sem("g_step")
        g_ps = sem("g_ps")
        g_act = sem("g_act")
        g_ready = sem("g_ready")
        xb_in = [sem(f"xb_in{k}") for k in range(4)]
        xn_ready = sem("xn_ready")
        idx_ready = sem("idx_ready")
        ag_zero = sem("ag_zero")
        ag_in = [sem(f"ag_in{k}") for k in range(2)]
        s_ready = sem("s_ready")
        xbt_ready = sem("xbt_ready")
        bhi_ready = sem("bhi_ready")
        blo_ready = sem("blo_ready")
        q_ready = sem("q_ready")
        comb_ready = sem("comb_ready")
        qmax_step = sem("qmax_step")
        q_exp = sem("q_exp")
        q_sums = sem("q_sums")
        q_scaled = sem("q_scaled")
        qt_ps = sem("qt_ps")
        qt_ready = sem("qt_ready")
        mix_ready = sem("mix_ready")
        sumsq_ready = sem("sumsq_ready")
        powb_in_ready = sem("powb_in_ready")
        powb_ready = sem("powb_ready")
        factors_ready = sem("factors_ready")
        mean_ready = sem("mean_ready")
        var_ready = sem("var_ready")
        mix_used = sem("mix_used")
        u_ready = sem("u_ready")
        x1_ready = sem("x1_ready")
        ln_step = sem("ln_step")
        o_ready = sem("o_ready")
        o_stored = [sem(f"o_stored{k}") for k in range(2)]
        t_step = sem("t_step")
        t_counts = sem("t_counts")
        t_total = sem("t_total")
        t_key = sem("t_key")
        params_ready = sem("params_ready")
        params_stored = sem("params_stored")
        hotl_ready = sem("hotl_ready")
        hotl_used = sem("hotl_used")
        part_ready = sem("part_ready")
        part_tr = sem("part_tr")
        part_in = sem("part_in")
        list_ps = sem("list_ps")
        cols_c = sem("cols_c")
        rows_in = [sem(f"rows_in{k}") for k in range(4)]
        pars_in = [sem(f"pars_in{k}") for k in range(4)]
        ln_ready = sem("ln_ready")
        ct_ready = sem("ct_ready")
        chi_ready = sem("chi_ready")
        clo_ready = sem("clo_ready")
        h_ps = sem("h_ps")
        h_act = sem("h_act")
        h_hi = sem("h_hi")
        h_lo = sem("h_lo")
        y_half = sem("y_half")
        y_ps = sem("y_ps")
        y_ready = sem("y_ready")
        scattered = [sem(f"scattered{k}") for k in range(4)]

        pool_count = nc.gpsimd.alloc_register("pool_count")
        dve_count = nc.vector.alloc_register("dve_count")

        def wait(eng, s, value, apart=False):
            if isinstance(value, int):
                if value > 0:
                    eng.wait_ge(s, value)
            elif apart or eng is nc.gpsimd:
                count = pool_count if eng is nc.gpsimd else dve_count
                eng.reg_mov(count, value)
                eng.wait_ge(constants_ready, 1)
                eng.wait_ge(s, count)
            else:
                eng.wait_ge(s, value)
                eng.wait_ge(constants_ready, 1)

        def rows_of(s, count=NB):
            return TAIL if s.is_last(count) else P

        def x_block(t, s):
            n = rows_of(s)
            rows = s.n * BLOCK
            return t[bass.ds(rows, n * J), :].rearrange("(p j) c -> p j c", j=J)

        LOOP_A = (4, 4 + (NB - 6 - 4) // 4 * 4)
        LOOP_B = (8, 8 + (NB - 4 - 8) // 4 * 4)
        LAST_B = NB + 5
        LOOP_C = (4, 4 + (NC - 3 - 4) // 4 * 4)
        N_WEIGHTS = 19

        block = ctx.enter_context(nc.Block())

        @block.sync
        def _(sp):
            def load(dst, src, spread=False):
                sp.dma_start(dst, src, allow_slow_non_contiguous=spread).then_inc(weights_in, 16)

            sp.wait_ge(pool_init, 5)
            n_full = FULL_LANES * NT
            for k, name in enumerate(("dst", "src")):
                sp.dma_start(ends[0:FULL_LANES, k], a[name][0:n_full].rearrange("(p t) -> p t", t=NT)).then_inc(edges_in, 16)
                sp.dma_start(ends[FULL_LANES:FULL_LANES + 1, k, 0:LAST_LANE], a[name][n_full:E].rearrange("(p t) -> p t", p=1)).then_inc(edges_in, 16)
            sp.dma_start(cut[0:FULL_LANES, :], a["edge_weight"][0:n_full].rearrange("(p t) -> p t", t=NT)).then_inc(edges_in, 16)
            sp.dma_start(cut[FULL_LANES:FULL_LANES + 1, 0:LAST_LANE], a["edge_weight"][n_full:E].rearrange("(p t) -> p t", p=1)).then_inc(edges_in, 16)
            load(st_qkv, a["L0_mix_w_qkv"].rearrange("(k p) n -> p k n", p=P))
            load(g_pre, a["L0_mix_g_pre"].rearrange("(k p) -> p k", p=P), spread=True)
            load(st_comb, a["L0_gnn_W_comb"][0:C, :].rearrange("(k p) n -> p k n", p=P))
            load(wb_f[:], a["L0_gnn_W_comb"][C:2 * C, :].rearrange("(k p) n -> p k n", p=P))
            load(wd_f[0:RBF, :], a["L0_gnn_W_dist"])
            load(wd_f[RBF:RBF + 1, :], a["L0_gnn_b_dist"].rearrange("(o n) -> o n", o=1))
            load(wo_f[:], a["L0_mix_w_out"])
            for k, name in enumerate(("L0_gnn_b_comb", "L0_mix_b_out")):
                load(st_bias[:, k, :], a[name].rearrange("(o n) -> o n", o=1).to_broadcast([P, C]))
            load(b2_r[:], a["L0_ffn_b2"].rearrange("(o n) -> o n", o=1).to_broadcast([P, C]))
            load(gout_r[:], a["L0_mix_g_out"].rearrange("(o n) -> o n", o=1).to_broadcast([P, C]))
            load(wr_r[:], a["L0_ffn_wr"].rearrange("n o -> o n").to_broadcast([P, C]))
            load(br_c[:], a["L0_ffn_br"].rearrange("(o n) -> o n", o=1).to_broadcast([P, 1]))
            load(b1_c[:], a["L0_ffn_b1"].rearrange("(m p) -> p m", p=P), spread=True)
            load(mem_k[:], a["L0_mix_mem_kv"][0].rearrange("h d m -> (h d) m"))
            load(mem_v[:], a["L0_mix_mem_kv"][1].rearrange("h d m -> (h d) m"))
            part112 = FULL_LANES // 16 * 16
            load(attr[0:part112], a["edge_attr_64"][0:part112 * NT, :].rearrange("(p t) c -> p t c", t=NT))
            load(attr[part112:FULL_LANES], a["edge_attr_64"][part112 * NT:n_full, :].rearrange("(p t) c -> p t c", t=NT))
            load(attr[FULL_LANES:FULL_LANES + 1, 0:LAST_LANE], a["edge_attr_64"][n_full:E, :].rearrange("(p t) c -> p t c", p=1))
            sp.dma_start(agg_tab.rearrange("(p r) c -> p r c", p=P), zero.unsqueeze(1).to_broadcast([P, TABLE // P, C])).then_inc(table_zeroed, 16)
            sp.wait_ge(slots_ready, 1)
            sp.dma_start(slot_tab.rearrange("(b p j) o -> p b (j o)", p=P, j=J), slot_i.rearrange("p (b j) -> p b j", j=J)).then_inc(slots_stored, 16)

            def load_a(s):
                if s.within(NB):
                    wait(sp, normed, (s - 3).n)
                    sp.dma_start(x_r[0:rows_of(s), s.ring(4)], x_block(x_d, s)).then_inc(x_in[s.ring(4)], 16)

            run_steps(sp, 0, NB - 1, *LOOP_A, load_a)

            sp.wait_ge(stage_a_done, 1)

            def traffic_b(s):
                ld, st = s + 3, s - 6
                if ld.within(NB):
                    wait(sp, u_ready, (ld - 3).n)
                    sp.dma_start(x_r[0:rows_of(ld), ld.ring(4)], x_block(x_d, ld)).then_inc(xb_in[ld.ring(4)], 16)
                if st.within(NB):
                    wait(sp, o_ready, (st + 1).n)
                    sp.dma_start(x_block(out, st), o_b[0:rows_of(st), st.ring(2)]).then_inc(o_stored[st.ring(2)], 16)

            run_steps(sp, -3, LAST_B, *LOOP_B, traffic_b)
            sp.wait_ge(params_ready, 1)
            sp.dma_start(st_w1, a["L0_ffn_w1"].rearrange("(k p) n -> p k n", p=P)).then_inc(ffn_in, 16)
            sp.dma_start(st_w2, a["L0_ffn_w2"].rearrange("(k p) n -> p k n", p=P)).then_inc(ffn_in, 16)
            sp.dma_start(row_tab.rearrange("(b p j) k -> p b (j k)", p=P, j=J), stat2[:].rearrange("p (b j) k -> p b (j k)", j=J)).then_inc(params_stored, 16)

        @block.gpsimd
        def _(pool):
            g = nc.gpsimd
            g.iota(ends[:, 0], pattern=[[0, NT]], base=N, channel_multiplier=0).then_inc(pool_init, 1)
            g.memset(cut, 0.0).then_inc(pool_init, 1)
            g.iota(ends[:, 1], pattern=[[0, NT]], base=0, channel_multiplier=0).then_inc(pool_init, 1)
            g.memset(attr, 0.0).then_inc(pool_init, 1)
            g.memset(zero, 0.0).then_inc(pool_init, 1)
            g.iota(iota_c[:], pattern=[[1, iota_c.shape[1]]], base=0, channel_multiplier=0, allow_small_or_imprecise_dtypes=True)
            g.iota(iota_h[:], pattern=[[1, iota_h.shape[1]]], base=0, channel_multiplier=0, allow_small_or_imprecise_dtypes=True)
            g.iota(lane_id[:], pattern=[[0, 1]], base=0, channel_multiplier=1, allow_small_or_imprecise_dtypes=True)
            g.iota(spare_row[:], pattern=[[0, 1]], base=SLOTS, channel_multiplier=1, allow_small_or_imprecise_dtypes=True)
            g.memset(half_neg[:], -0.5)
            g.memset(ones_b[:], 1.0)
            g.memset(ones[:], 1.0).then_inc(constants_ready, 1)
            pool.wait_ge(constants_ready, 1)
            g.affine_select(out=ident[:], in_=ones[:], compare_op=ALU.is_equal, fill=0.0, base=0, pattern=[[-1, P]], channel_multiplier=1)
            g.affine_select(out=before[:], in_=ones[:], compare_op=ALU.is_gt, fill=0.0, base=0, pattern=[[1, P]], channel_multiplier=-1)
            g.affine_select(out=earlier[:], in_=ones[:], compare_op=ALU.is_gt, fill=0.0, base=0, pattern=[[-1, P]], channel_multiplier=1)
            g.affine_select(out=same_head[:].rearrange("p (h d) -> p h d", d=DH), in_=ones[:].rearrange("p (h d) -> p h d", d=DH),
                            compare_op=ALU.is_ge, fill=0.0, base=0, pattern=[[-DH, HEADS], [0, DH]], channel_multiplier=1).then_inc(constants_ready, 1)
            pool.wait_ge(constants_ready, 2)
            g.affine_select(out=same_head[:].rearrange("p (h d) -> p h d", d=DH), in_=same_head[:].rearrange("p (h d) -> p h d", d=DH),
                            compare_op=ALU.is_ge, fill=0.0, base=DH - 1, pattern=[[DH, HEADS], [0, DH]], channel_multiplier=-1).then_inc(constants_ready, 1)

            pool.wait_ge(weights_in, 16 * N_WEIGHTS)
            for k in range(2):
                ins = g.tensor_tensor(st_comb[:, k, k * P:(k + 1) * P], st_comb[:, k, k * P:(k + 1) * P], ident[:], ALU.add)
            ins.then_inc(comb_plus, 1)
            pool.wait_ge(comb_plus, 1)
            for k in range(2):
                pool.wait_ge(bias_act, 2 * k + 2)
                g.tensor_tensor(sp_bias[:, k], sp_bias[:, 0] if k else st_bias, bias_tmp[:], ALU.subtract).then_inc(bias_pool, 1)
                pool.wait_ge(bias_pool, k + 1)
            pool.wait_ge(halves_ready, 1)
            for parts, whole in ((wq_s, st_qkv[:, :, 0:P]), (wk_s, st_qkv[:, :, P:2 * P]), (wc_s, st_comb)):
                ins = g.tensor_tensor(parts[:, 1], whole, parts[:, 0], ALU.subtract)
            ins.then_inc(weights_ready, 1)
            pool.wait_ge(weights_ready, 1)
            pool.wait_ge(slots_stored, 16)
            pool.wait_ge(table_zeroed, 16)

            def step_a(s):
                nxt = s + 2
                if nxt.ring(2) == 0 and nxt.within(NB):
                    k = nxt.ring(4) // 2
                    wait(pool, pow_in_ready, nxt.of(1, 2) + 1)
                    g.tensor_tensor(pow_out[:, k], pow_in[:, k], half_neg[:].rearrange("p (a b) -> p a b", a=2), ALU.pow).then_inc(pow_ready, 1)
                t = s + 2
                if t.within(NT):
                    k = t.ring(4)
                    wait(pool, ends_ready, t.n + 1)
                    wait(pool, emb_in[k], t.of(16, 4))
                    wait(pool, lead_step, (t - 3).of(4, 1))
                    g.indirect_dma_start(kind_c[:, k:k + 1], None, a["node_type_100"].rearrange("(n o) -> n o", o=1),
                                         bass.IndirectOffsetOnAxis(ap=end_c[:, k, 1:2], axis=0), bounds_check=N - 1, oob_is_err=False).then_inc(kinds_in[k], 16)
                    g.indirect_dma_start(slot_c[:, k:k + 1], None, slot_tab,
                                         bass.IndirectOffsetOnAxis(ap=end_c[:, k, 0:1], axis=0), bounds_check=NB * BLOCK - 1, oob_is_err=False).then_inc(slots_in[k], 16)
                t = s + 1
                if t.within(NT):
                    k = t.ring(4)
                    wait(pool, kinds_in[k], t.of(16, 4) + 16)
                    wait(pool, msg_ready, (t - 3).n)
                    g.indirect_dma_start(emb[:, k], None, a["L0_gnn_embed_table"],
                                         bass.IndirectOffsetOnAxis(ap=kind_c[:, k:k + 1], axis=0), bounds_check=SPECIES - 1, oob_is_err=False).then_inc(emb_in[k], 16)
                t = s - 2
                if t.within(NT):
                    wait(pool, contrib_ready, t.n + 1)
                    wait(pool, added, t.of(16, 1))
                    g.indirect_dma_start(agg_tab, bass.IndirectOffsetOnAxis(ap=goal[:, t.ring(4):t.ring(4) + 1], axis=0), contrib[:, t.ring(2)], None,
                                         bounds_check=TABLE - 1, compute_op=ALU.add).then_inc(added, 16)

            run_steps(pool, -2, NB + 1, *LOOP_A, step_a)
            pool.wait_ge(added, 16 * NT)
            pool.wait_ge(stage_a_done, 1)

            def step_b(s):
                t = s + 1
                if t.within(NB):
                    k = t.ring(2)
                    wait(pool, s_ready, (t - 1).n)
                    g.memset(ag[:, k], 0.0).then_inc(ag_zero, 1)
                    wait(pool, ag_zero, t.n + 1)
                    wait(pool, idx_ready, t.n + 1)
                    for j in range(J):
                        g.indirect_dma_start(ag[:, k, j], None, agg_tab, bass.IndirectOffsetOnAxis(ap=idx_b[:, t.ring(4), j:j + 1], axis=0),
                                             bounds_check=TABLE - 1, oob_is_err=False).then_inc(ag_in[k], 16)
                if s.within(NB):
                    n, k = rows_of(s), s.ring(2)
                    wait(pool, xn_ready, s.n + 1)
                    wait(pool, ag_in[k], s.of(16 * J, 2) + 16 * J)
                    g.tensor_tensor(x_r[0:n, s.ring(4)], x_r[0:n, s.ring(4)], ag[0:n, k], ALU.add).then_inc(s_ready, 1)
                t = s - 1
                if t.within(NB):
                    n, k = rows_of(t), t.ring(2)
                    wait(pool, q_sums, 2 * t.n + 2)
                    qv = q_e[0:n, k].rearrange("p (h d) -> p h d", d=DH)
                    g.tensor_tensor(qv, qv, q_inv[0:n, k].unsqueeze(2).to_broadcast([n, 16, DH]), ALU.mult).then_inc(q_scaled, 1)
                t = s - 3
                if t.within(NB + 2):
                    k = (t + 1).ring(2)
                    wait(pool, powb_in_ready, t.n + 1)
                    g.tensor_tensor(powb_out[:, k], powb_in[:, k], half_neg[:, 0:2 * J].rearrange("p (a b) -> p a b", a=2), ALU.pow).then_inc(powb_ready, 1)

            run_steps(pool, -1, LAST_B, *LOOP_B, step_b)

            pool.wait_ge(ffn_upper, 1)
            g.tensor_tensor(w1_s[:, 1], st_w1, w1_s[:, 0], ALU.subtract)
            g.tensor_tensor(w2_s[:, 1], st_w2, w2_s[:, 0], ALU.subtract).then_inc(ffn_ready, 1)
            pool.wait_ge(params_stored, 16)
            for k in range(2):
                pool.wait_ge(o_stored[k], 16 * (NB // 2))

            def step_c(s):
                t = s + 2
                if t.within(NC):
                    k = t.ring(4)
                    wait(pool, cols_c, t.n + 1)
                    wait(pool, scattered[k], t.of(16 * J, 4))
                    for j in range(J):
                        g.indirect_dma_start(g_r[:, k, j], None, out, bass.IndirectOffsetOnAxis(ap=row_c[:, k, j:j + 1], axis=0),
                                             bounds_check=N - 1, oob_is_err=False).then_inc(rows_in[k], 16)
                        g.indirect_dma_start(par[:, k, j], None, row_tab, bass.IndirectOffsetOnAxis(ap=row_c[:, k, j:j + 1], axis=0),
                                             bounds_check=N - 1, oob_is_err=False).then_inc(pars_in[k], 16)
                t = s - 1
                if t.within(NC):
                    k = t.ring(4)
                    wait(pool, y_ready, t.n + 1)
                    for j in range(J):
                        g.indirect_dma_start(out, bass.IndirectOffsetOnAxis(ap=row_c[:, k, j:j + 1], axis=0), g_r[:, k, j], None,
                                             bounds_check=N - 1, oob_is_err=False).then_inc(scattered[k], 16)

            run_steps(pool, -2, NC, *LOOP_C, step_c)
            for k in range(4):
                pool.wait_ge(scattered[k], 16 * J * len(range(k, NC, 4)))

        @block.scalar
        def _(act):
            sc = nc.scalar
            act.wait_ge(angle_ready, 1)
            sc.activation(cut2, cut2, ACT.Sin).then_inc(cos_ready, 1)
            act.wait_ge(weights_in, 16 * N_WEIGHTS)
            sc.activation(st_bias, st_bias, ACT.Copy, scale=1.0 / 32).then_inc(bias_act, 1)
            act.wait_ge(bias_act, 1)
            sc.copy(bias_b[0:32], st_bias[0:32])
            sc.copy(bias_tmp[:], st_bias).then_inc(bias_act, 1)
            act.wait_ge(bias_pool, 1)
            sc.copy(bias_b[32:64], sp_bias[32:64, 0])
            sc.activation(bias_b[96:128], st_bias[96:128], ACT.Copy, scale=0.0).then_inc(bias_act, 1)
            sc.copy(bias_tmp[:], sp_bias[:, 0]).then_inc(bias_act, 1)
            for k in range(2):
                ins = sc.activation(st_qkv[:, k], st_qkv[:, k], ACT.Copy, scale=g_pre[:, k:k + 1])
            ins.then_inc(qkv_scaled, 1)
            act.wait_ge(qkv_scaled, 1)
            act.wait_ge(comb_plus, 1)
            sc.copy(wv_f[:], st_qkv[:, :, 2 * P:3 * P])
            for parts, whole in ((wq_s, st_qkv[:, :, 0:P]), (wk_s, st_qkv[:, :, P:2 * P]), (wc_s, st_comb)):
                ins = sc.copy(parts[:, 0], whole)
            ins.then_inc(halves_ready, 1)
            act.wait_ge(bias_pool, 2)
            sc.copy(bias_b[64:96], sp_bias[64:96, 1]).then_inc(bias_act, 1)

            def step_a(s):
                b = s - 2
                if b.within(NB):
                    n = rows_of(b)
                    wait(act, et_ready, b.n + 1)
                    wait(act, sums_ready, (b - 1).n)
                    sc.copy(e_n[0:n, b.ring(2)], psum[3][0:n, :]).then_inc(en_ready, 1)
                t = s
                if t.within(NT):
                    wait(act, attr_tr, t.n + 1)
                    wait(act, filter_ready, (t - 1).n)
                    sc.copy(attr_t[0:RBF, t.ring(2)], psum[5][0:RBF, 0:P]).then_inc(attr_t_ready, 1)
                if s.within(NB):
                    n = rows_of(s)
                    wait(act, xt_ready, s.n + 1)
                    wait(act, keys_ready, (s - 1).n)
                    for k in range(2):
                        ins = sc.copy(xs_a[:, s.ring(2), 0, k].rearrange("p (j r) -> p j r", j=J)[:, :, 0:n],
                                      psum[k][:].rearrange("p (j r) -> p j r", j=J)[:, :, 0:n])
                    ins.then_inc(xhi_ready, 1)
                b = s + 1
                if b.within(NB):
                    n, k4, h = rows_of(b), b.ring(4), b.ring(2) * J
                    pr = pair[:, k4 // 2]
                    wait(act, scale_step, b.of(5, 2) + 5)
                    wait(act, x_in[k4], b.of(16, 4) + 16)
                    wait(act, sums_ready, (b - 3).n)
                    for j in range(J):
                        ins = sc.activation(xr[0:n, k4, j], x_r[0:n, k4, j], ACT.Identity, scale=pr[0:n, 7, h + j:h + j + 1], bias=pr[0:n, 9, h + j:h + j + 1])
                    ins.then_inc(normed, 1)
                t = s - 1
                if t.within(NT):
                    wait(act, merged, t.n + 1)
                    sc.copy(msg_t[:, t.ring(2)], psum[6][:, 0:C]).then_inc(merged_t, 1)
                b = s - 1
                if b.within(NB):
                    w = rows_of(b) * J
                    k = b.ring(4)
                    wait(act, keys_ready, b.n + 1)
                    wait(act, max_step, 3 * b.n + 3)
                    wait(act, et_ready, (b - 1).n)
                    sc.activation(e_t[:, b.ring(2), 0:w], psum[2][:, 0:w], ACT.Exp, bias=neg_max[:, k:k + 1], accum_out=row_sum[:, k:k + 1])
                    sc.activation(decay[:, k:k + 1], run_max[:, (k - 1) % 4:(k - 1) % 4 + 1], ACT.Exp, bias=neg_max[:, k:k + 1]).then_inc(exp_ready, 1)
                t = s - 1
                if t.within(NT):
                    wait(act, contrib_ps, t.n + 1)
                    wait(act, added, (t - 1).of(16, 1))
                    sc.copy(contrib[:, t.ring(2)], psum[6][:, C:2 * C]).then_inc(contrib_ready, 1)

            run_steps(act, -1, NB + 1, *LOOP_A, step_a)

            act.wait_ge(g_step, 2)
            sc.activation(mem_e, mem_k[:], ACT.Exp, bias=neg_max[:, (NB - 1) % 4:(NB - 1) % 4 + 1], accum_out=small[:, 8:9]).then_inc(g_act, 1)

            def step_b(s):
                b = s - 3
                if b.within(NB):
                    n = rows_of(b)
                    wait(act, qt_ps, b.n + 1)
                    wait(act, mix_ready, (b - 1).n)
                    sc.copy(q_t[:, b.ring(2)].rearrange("p (j r) -> p j r", j=J)[:, :, 0:n], psum[3][:].rearrange("p (j r) -> p j r", j=J)[:, :, 0:n]).then_inc(qt_ready, 1)
                if s.within(NB):
                    n = rows_of(s)
                    wait(act, xbt_ready, s.n + 1)
                    wait(act, comb_ready, (s - 1).n)
                    for k in range(2):
                        ins = sc.copy(xs_b[:, s.ring(2), 0, k].rearrange("p (j r) -> p j r", j=J)[:, :, 0:n],
                                      psum[k][:].rearrange("p (j r) -> p j r", j=J)[:, :, 0:n])
                    ins.then_inc(bhi_ready, 1)
                b = s + 1
                if b.within(NB):
                    n, k = rows_of(b), b.ring(2)
                    wait(act, xb_in[b.ring(4)], b.of(16, 4) + 16)
                    wait(act, xbt_ready, (b - 1).n)
                    for j in range(J):
                        col = b.n * J + j
                        ins = sc.activation(xn[0:n, k, j], x_r[0:n, b.ring(4), j], ACT.Identity, scale=inv_sd[0:n, bass.ds(col, 1)], bias=shift[0:n, bass.ds(col, 1)])
                    ins.then_inc(xn_ready, 1)
                b = s - 5
                if b.within(NB):
                    n = rows_of(b)
                    wait(act, mean_ready, b.n + 1)
                    for j in range(J):
                        ins = sc.activation(var_junk[0:n, b.ring(2), j], x1[0:n, b.ring(4), j], ACT.Square, bias=ln_b[0:n, b.ring(2), 0, j:j + 1],
                                            accum_out=varsum[0:n, b.ring(4), j:j + 1])
                    ins.then_inc(var_ready, 1)
                b = s - 1
                if b.within(NB):
                    n, k = rows_of(b), b.ring(2)
                    wait(act, qmax_step, 2 * b.n + 2)
                    for j in range(J):
                        col = b.n * J + j
                        ins = sc.activation(q_e[0:n, k, j * P:(j + 1) * P], q_e[0:n, k, j * P:(j + 1) * P], ACT.Exp,
                                            scale=inv_rms[0:n, bass.ds(col, 1)])
                    ins.then_inc(q_exp, 1)
                b = s - 3
                if b.within(NB):
                    n = rows_of(b)
                    wait(act, mix_ready, b.n + 1)
                    for j in range(J):
                        ins = sc.activation(sq_junk[0:n, j], psum[6 + j // 2][0:n, j % 2 * C:(j % 2 + 1) * C], ACT.Square,
                                            accum_out=sumsq[0:n, b.ring(4), j:j + 1])
                    ins.then_inc(sumsq_ready, 1)
                b = s - 6
                if b.within(NB):
                    n, k = rows_of(b), b.ring(2)
                    wait(act, factors_ready, b.n + 1)
                    wait(act, o_stored[k], b.of(16, 2))
                    for j in range(J):
                        ins = sc.activation(o_b[0:n, k, j], x1[0:n, b.ring(4), j], ACT.Identity, scale=mix_r[0:n, b.ring(4), 2, j:j + 1], bias=mix_r[0:n, b.ring(4), 3, j:j + 1])
                    ins.then_inc(o_ready, 1)

            run_steps(act, -1, LAST_B, *LOOP_B, step_b)

            act.wait_ge(ffn_in, 32)
            sc.copy(w1_s[:, 0], st_w1)
            sc.copy(w2_s[:, 0], st_w2).then_inc(ffn_upper, 1)

            def step_c(s):
                if s.within(NC):
                    for m in range(FK):
                        wait(act, h_ps, s.of(FK, 1) + m + 1)
                        wait(act, h_lo, s.of(FK, 1) + m - 3)
                        sc.activation(h_f[:, m % 4], psum[2 + m % 4][:], ACT.Gelu_apprx_tanh, bias=b1_c[:, m:m + 1]).then_inc(h_act, 1)
                b = s + 1
                if b.within(NC):
                    wait(act, ct_ready, b.n + 1)
                    wait(act, h_ps, (b - 1).of(FK, 1))
                    for k in range(2):
                        ins = sc.copy(xs_c[:, b.ring(2), 0, k], psum[k][:])
                    ins.then_inc(chi_ready, 1)

            run_steps(act, -1, NC - 1, *LOOP_C, step_c)

        @block.vector
        def _(dve):
            v = nc.vector

            def split(parts, whole, done=None):
                v.tensor_copy(parts[0], whole).then_inc(dve_init, 1)
                split.count += 1
                dve.wait_ge(dve_init, split.count)
                ins = v.tensor_tensor(parts[1], whole, parts[0], ALU.subtract)
                return ins

            split.count = 0

            def chain(ins):
                ins.then_inc(dve_init, 1)
                split.count += 1
                dve.wait_ge(dve_init, split.count)

            def ranks(mask, rank_out, tmp, turn):
                m3 = mask.rearrange("p (b j) -> p b j", j=J)
                r3 = rank_out.rearrange("p (b j) -> p b j", j=J)
                v.tensor_reduce(tmp[:, 0], m3, AX.X, ALU.add).then_inc(rank_in, 1)
                dve.wait_ge(rank_sums, turn)
                v.tensor_tensor_scan(tmp[:, 1], ones[:, 0:1].to_broadcast([P, NB]), psum[5][:, 0:NB], 0.0, ALU.mult, ALU.add).then_inc(rank_step, 1)
                dve.wait_ge(rank_step, 6 * turn - 5)
                v.tensor_tensor(tmp[:, 2], tmp[:, 1], psum[5][:, 0:NB], ALU.subtract).then_inc(rank_step, 1)
                dve.wait_ge(rank_step, 6 * turn - 4)
                v.tensor_tensor(r3[:, :, 0], tmp[:, 2], psum[4][:, 0:NB], ALU.add).then_inc(rank_step, 1)
                for j in range(1, J):
                    dve.wait_ge(rank_step, 6 * turn - 4 + j)
                    v.tensor_tensor(r3[:, :, j], r3[:, :, j - 1], m3[:, :, j - 1], ALU.add).then_inc(rank_step, 1)
                dve.wait_ge(rank_step, 6 * turn)

            v.memset(small[:], 0.0)
            v.memset(attr_t, 1.0)
            v.memset(attr_c, 0.0)
            v.memset(bn, 0.0)
            v.memset(acc, 0.0)
            v.memset(denom, 0.0)
            v.memset(inv_sd[:], 0.0)
            v.memset(inv_rms[:], 0.0)
            v.memset(shift[:], 0.0)
            v.memset(stat2[:], 0.0)
            chain(v.memset(dot2[:], 0.0))
            dve.wait_ge(constants_ready, 3)
            dve.wait_ge(edges_in, 96)
            chain(v.tensor_scalar(cut2, cut, -1.0, None, ALU.mult))
            chain(v.tensor_tensor(cut2, cut2, cut, ALU.max))
            chain(v.tensor_scalar(cut2, cut2, CUTOFF, -float(np.pi) / CUTOFF, ALU.min, ALU.mult))
            v.tensor_scalar(cut2, cut2, float(np.pi) / 2, None, ALU.add).then_inc(angle_ready, 1)
            chain(v.tensor_scalar(ei[:, 0], ends[:, 0], 2, 127, ALU.logical_shift_right, ALU.bitwise_and))
            chain(v.tensor_scalar(ei[:, 1], ends[:, 0], 9, 2, ALU.logical_shift_right, ALU.logical_shift_left))
            chain(v.tensor_scalar(ei[:, 2], ends[:, 0], 3, None, ALU.bitwise_and))
            chain(v.tensor_tensor(ei[:, 1], ei[:, 1], ei[:, 2], ALU.bitwise_or))
            v.tensor_copy(dst_f, ends[:, 0])
            v.tensor_copy(dst_p, ei[:, 0])
            chain(v.tensor_copy(dst_c, ei[:, 1]))

            def hot(t, k, used):
                wait(dve, hot_used, used)
                v.tensor_scalar(hot_p[:, k], iota_h[:, 0:P], dst_p[:, bass.ds(t, 1)], None, ALU.is_equal)
                v.tensor_scalar(hot_c[:, k], iota_h[:, 0:COLS], dst_c[:, bass.ds(t, 1)], None, ALU.is_equal).then_inc(hot_ready, 1)

            PEEL_E = 4 + NT % 4
            for t in range(PEEL_E):
                hot(t, t % 4, t - 3)
            with dve.Fori(0, (NT - PEEL_E) // 4) as i:
                for k in range(4):
                    hot(i * 4 + (PEEL_E + k), (PEEL_E + k) % 4, i * 4 + (PEEL_E + k - 3))
            dve.wait_ge(counted, 1)
            chain(v.tensor_scalar(touched, psum[7][:, 0:COLS], 0.5, None, ALU.is_gt))
            ranks(touched, rank, rk, 1)
            chain(v.tensor_scalar(count, rank, FAR, None, ALU.subtract))
            chain(v.tensor_tensor(count, count, touched, ALU.mult))
            v.tensor_scalar(agg_row[:], count, FAR, None, ALU.add)
            v.tensor_copy(slot_i, rank).then_inc(slots_ready, 1)

            dve.wait_ge(weights_in, 16 * N_WEIGHTS)
            chain(v.tensor_reduce(wr_sum[:], wr_r[:], AX.X, ALU.add))
            chain(v.tensor_reduce(run_max[:, 3:4], mem_k[:], AX.X, ALU.max))
            dve.wait_ge(cos_ready, 1)
            chain(v.tensor_scalar(cut2, cut2, 1.0, 0.5, ALU.add, ALU.mult))
            chain(v.tensor_scalar(cut, cut, CUTOFF, None, ALU.is_lt))
            chain(v.tensor_tensor(cut2, cut2, cut, ALU.mult))

            def step_a(s):
                b = s - 3
                if b.within(NB):
                    kb = b.ring(4)
                    wait(dve, exp_ready, b.n + 1)
                    wait(dve, sums_ready, b.n + 1)
                    wait(dve, acc_step, b.n)
                    v.scalar_tensor_tensor(denom, denom, decay[:, kb:kb + 1], row_sum[:, kb:kb + 1], ALU.mult, ALU.add)
                    v.scalar_tensor_tensor(acc, acc, decay[:, kb:kb + 1], psum[4][:, 0:C], ALU.mult, ALU.add).then_inc(acc_step, 1)
                b = s + 3
                if b.within(NB):
                    n = rows_of(b)
                    wait(dve, x_in[b.ring(4)], b.of(16, 4) + 16)
                    for j in range(J):
                        ins = v.bn_stats(bn[0:n, 4 * b.ring(2) + j], x_r[0:n, b.ring(4), j])
                    if b.ring(2) == 1:
                        ins.then_inc(stats_step, 1)
                q = s + 2
                stats = q.ring(2) == 0 and q.within(NB)
                kq, at = q.ring(4) // 2, q.of(5, 2)
                pq = pair[:, kq]
                b = s - 1
                if b.within(NB):
                    w, kb = rows_of(b) * J, b.ring(4)
                    wait(dve, keys_ready, b.n + 1)
                    v.tensor_reduce(blk_max[:, kb:kb + 1], psum[2][:, 0:w], AX.X, ALU.max).then_inc(max_step, 1)
                if stats:
                    wait(dve, stats_step, at + 1)
                    v.tensor_tensor(pq[:, 0], bn[:, :, 1], bn[:, :, 4], ALU.add)
                    v.tensor_tensor(pq[:, 1], bn[:, :, 1], bn[:, :, 4], ALU.subtract)
                    v.tensor_tensor(pq[:, 2], bn[:, :, 2], bn[:, :, 5], ALU.add).then_inc(stats_step, 1)
                t = s + 1
                if t.within(NT):
                    k = t.ring(2)
                    wait(dve, attr_tr, (t - 1).n)
                    wait(dve, dst_row, (t - 1).n)
                    v.tensor_copy(attr_c[:, k, 0:RBF], attr[:, bass.ds(t.n, 1), :])
                    v.tensor_scalar(diag[:, k], ident[:], dst_f[:, bass.ds(t.n, 1)], None, ALU.mult).then_inc(edge_cols, 1)
                if stats:
                    wait(dve, stats_step, at + 2)
                    v.scalar_tensor_tensor(pq[:, 3], pq[:, 1], 0.25, pq[:, 1], ALU.mult, ALU.mult).then_inc(stats_step, 1)
                if (s - 1).within(NB):
                    wait(dve, max_step, 3 * (s - 1).n + 1)
                    p_ = (kb - 1) % 4
                    v.tensor_tensor(run_max[:, kb:kb + 1], blk_max[:, kb:kb + 1], run_max[:, p_:p_ + 1], ALU.max).then_inc(max_step, 1)
                if stats:
                    wait(dve, stats_step, at + 3)
                    v.scalar_tensor_tensor(pq[:, 4], pq[:, 2], 1.0 / C, pq[:, 3], ALU.mult, ALU.add).then_inc(stats_step, 1)
                t = s + 3
                if t.within(NT):
                    wait(dve, kinds_in[t.ring(4)], t.of(16, 4))
                    wait(dve, slots_in[t.ring(4)], t.of(16, 4))
                    v.tensor_copy(end_c[:, t.ring(4)], ends[:, :, bass.ds(t.n, 1)].rearrange("p a o -> p (a o)")).then_inc(ends_ready, 1)
                if stats:
                    wait(dve, stats_step, at + 4)
                    v.tensor_scalar(pow_in[:, kq, 0], pq[:, 4], LN_EPS, None, ALU.add).then_inc(stats_step, 1)
                if (s - 1).within(NB):
                    wait(dve, max_step, 3 * (s - 1).n + 2)
                    v.tensor_scalar(neg_max[:, kb:kb + 1], run_max[:, kb:kb + 1], -1.0, None, ALU.mult).then_inc(max_step, 1)
                if stats:
                    wait(dve, stats_step, at + 5)
                    v.reciprocal(pq[:, 5], pow_in[:, kq, 0]).then_inc(scale_step, 1)
                b = s + 1
                first = b.ring(2) == 0 and b.within(NB)
                if first:
                    k, at, cols = b.ring(4) // 2, b.of(5, 2), bass.ds(b.n * J, 2 * J)
                    pr = pair[:, k]
                    wait(dve, pow_ready, b.of(1, 2) + 1)
                    wait(dve, normed, (b - 2).n)
                    v.tensor_tensor(pr[:, 7], pow_out[:, k, 0], pow_out[:, k, 1], ALU.mult)
                    v.scalar_tensor_tensor(pr[:, 8], pr[:, 0], -0.5, pow_out[:, k, 0], ALU.mult, ALU.mult).then_inc(scale_step, 1)
                    v.tensor_copy(inv_sd[:, cols], pow_out[:, k, 0])
                    v.tensor_copy(inv_rms[:, cols], pow_out[:, k, 1])
                    wait(dve, scale_step, at + 3)
                    v.tensor_tensor(pr[:, 9], pr[:, 8], pow_out[:, k, 1], ALU.mult).then_inc(scale_step, 1)
                    v.tensor_copy(shift[:, cols], pr[:, 8]).then_inc(scale_step, 1)
                if stats:
                    wait(dve, scale_step, at + 1)
                    v.tensor_tensor(pq[:, 6], pq[:, 5], pq[:, 4], ALU.mult).then_inc(scale_step, 1)
                if s.within(NB):
                    n = rows_of(s)
                    wait(dve, xt_ready, s.n + 1)
                    wait(dve, xhi_ready, s.n + 1)

                    def part(t):
                        return t.rearrange("p (j r) -> p j r", j=J)[:, :, 0:n]
                    for k in range(2):
                        ins = v.tensor_tensor(part(xs_a[:, s.ring(2), 1, k]), part(psum[k][:]), part(xs_a[:, s.ring(2), 0, k]), ALU.subtract)
                    ins.then_inc(xlo_ready, 1)
                if stats:
                    wait(dve, scale_step, at + 2)
                    v.tensor_scalar(pow_in[:, kq, 1], pq[:, 6], RMS_FLOOR ** 2 / C, None, ALU.max).then_inc(pow_in_ready, 1)
                t = s
                k, k4 = t.ring(2), t.ring(4)
                edges = t.within(NT)
                if edges:
                    wait(dve, dst_row, t.n + 1)
                    wait(dve, merged, (t - 1).n)
                    v.tensor_scalar(equal[:, k], psum[7][:, 0:P], dst_f[:, bass.ds(t.n, 1)], None, ALU.is_equal).then_inc(equal_ready, 1)
                if edges:
                    wait(dve, slots_in[k4], t.of(16, 4) + 16)
                    v.tensor_tensor(lead[:, k, 1:2], spare_row[:], slot_c[:, k4:k4 + 1], ALU.subtract).then_inc(lead_step, 1)
                    wait(dve, equal_ready, t.n + 1)
                    v.tensor_tensor_reduce(junk_p, equal[:, k], earlier[:], 1.0, 0.0, ALU.mult, ALU.add, lead[:, k, 0:1]).then_inc(lead_step, 1)
                if edges:
                    wait(dve, lead_step, 4 * t.n + 2)
                    v.tensor_scalar(lead[:, k, 2:3], lead[:, k, 0:1], 0.5, None, ALU.is_gt).then_inc(lead_step, 1)
                if edges:
                    wait(dve, lead_step, 4 * t.n + 3)
                    wait(dve, added, (t - 3).of(16, 1))
                    v.scalar_tensor_tensor(goal[:, k4:k4 + 1], lead[:, k, 1:2], lead[:, k, 2:3], slot_c[:, k4:k4 + 1], ALU.mult, ALU.add).then_inc(lead_step, 1)
                if edges:
                    wait(dve, filter_ready, t.n + 1)
                    wait(dve, emb_in[k4], t.of(16, 4) + 16)
                    v.scalar_tensor_tensor(msg[:, k], psum[5][:, 0:C], cut2[:, bass.ds(t.n, 1)], emb[:, k4], ALU.mult, ALU.mult).then_inc(msg_ready, 1)

            run_steps(dve, -3, NB + 2, *LOOP_A, step_a)

            dve.wait_ge(acc_step, NB)
            v.tensor_copy(small[:, 0:1], denom).then_inc(g_step, 1)
            dve.wait_ge(exp_ready, NB)
            dve.wait_ge(g_step, 1)
            v.tensor_copy(small[:, 1:2], small[:, 0:1]).then_inc(g_step, 1)
            dve.wait_ge(g_ps, 1)
            v.tensor_copy(acc_t, psum[0][:, 0:C].rearrange("p (k n) -> p k n", k=2))
            dve.wait_ge(g_ps, 2)
            v.tensor_copy(mem_t[0:MEM], psum[1][0:MEM, 0:2 * P].rearrange("p (k n) -> p k n", k=2)).then_inc(g_step, 1)
            dve.wait_ge(g_act, 1)
            v.tensor_tensor(small[:, 2:3], small[:, 0:1], small[:, 8:9], ALU.add).then_inc(g_step, 1)
            dve.wait_ge(g_step, 4)
            v.reciprocal(small[:, 3:4], small[:, 2:3]).then_inc(g_step, 1)
            dve.wait_ge(g_step, 5)
            v.tensor_scalar(small[:, 4:5], small[:, 3:4], float(DH) ** -0.5, None, ALU.mult).then_inc(g_step, 1)
            dve.wait_ge(g_ps, 3)
            v.tensor_tensor(ctx_t, psum[2][:, 0:P], same_head[:], ALU.mult).then_inc(g_step, 1)
            dve.wait_ge(g_step, 7)
            dve.wait_ge(g_ps, 4)
            v.tensor_scalar(g_f[:], psum[3][:, 0:C], small[:, 4:5], None, ALU.mult).then_inc(g_ready, 1)
            dve.wait_ge(added, 16 * NT)
            v.tensor_copy(small[:, 5:6], small[:, 4:5]).then_inc(stage_a_done, 1)

            def step_b(s):
                b = s + 2
                if b.within(NB):
                    k = b.ring(4)
                    wait(dve, s_ready, (b - 3).n)
                    v.tensor_copy(idx_b[:, k], agg_row[:, bass.ds(b.n * J, J)]).then_inc(idx_ready, 1)
                b = s - 2
                if b.within(NB):
                    n = rows_of(b)
                    wait(dve, comb_ready, b.n + 1)
                    wait(dve, s_ready, b.n + 1)
                    for h in range(2):
                        sv = slice(2 * h, 2 * h + 2)
                        ins = v.tensor_tensor(s_b[0:n, b.ring(4), sv], psum[4 + h][0:n, :].rearrange("p (j c) -> p j c", j=2), x_r[0:n, b.ring(4), sv], ALU.add)
                    ins.then_inc(u_ready, 1)
                b = s - 4
                if b.within(NB):
                    n = rows_of(b)
                    wait(dve, powb_ready, b.n + 1)
                    wait(dve, o_ready, (b - 3).n)
                    for j in range(J):
                        ins = v.scalar_tensor_tensor(x1[0:n, b.ring(4), j], psum[6 + j // 2][0:n, j % 2 * C:(j % 2 + 1) * C], powb_out[0:n, (b + 1).ring(2), 0, j:j + 1],
                                                     gout_r[0:n], ALU.mult, ALU.mult)
                    ins.then_inc(mix_used, 1)
                b = s - 6
                if b.within(NB):
                    cols = bass.ds(b.n * J, J)
                    mr, less, rr = mix_r[:, b.ring(4)], ln_b[:, b.ring(2), 0], powb_out[:, (b + 1).ring(2), 1]
                    wait(dve, powb_ready, b.n + 3)
                    v.tensor_scalar(mr[:, 2], rr, 1.0, None, ALU.add)
                    v.tensor_tensor(mr[:, 3], less, rr, ALU.mult).then_inc(factors_ready, 1)
                    v.tensor_copy(stat2[:, cols, 1], rr)
                if s.within(NB):
                    n = rows_of(s)
                    wait(dve, xbt_ready, s.n + 1)
                    wait(dve, bhi_ready, s.n + 1)

                    def part(t):
                        return t.rearrange("p (j r) -> p j r", j=J)[:, :, 0:n]
                    for k in range(2):
                        ins = v.tensor_tensor(part(xs_b[:, s.ring(2), 1, k]), part(psum[k][:]), part(xs_b[:, s.ring(2), 0, k]), ALU.subtract)
                    ins.then_inc(blo_ready, 1)
                b = s - 1
                if b.within(NB):
                    n, k = rows_of(b), b.ring(2)
                    wait(dve, q_ready, b.n + 1)
                    q4 = psum[2][0:n, :].rearrange("p (h d) -> p h d", d=DH)
                    v.tensor_reduce(q_max[0:n, k], q4, AX.X, ALU.max).then_inc(qmax_step, 1)
                    wait(dve, qmax_step, 2 * b.n + 1)
                    wait(dve, qt_ps, (b - 1).n)
                    v.tensor_tensor(q_e[0:n, k].rearrange("p (h d) -> p h d", d=DH), q4, q_max[0:n, k].unsqueeze(2).to_broadcast([n, 16, DH]), ALU.subtract).then_inc(qmax_step, 1)
                b = s - 4
                if b.within(NB):
                    n = rows_of(b)
                    wait(dve, mix_used, b.n + 1, apart=True)
                    for j in range(J):
                        row = x1[0:n, b.ring(4), j]
                        ins = v.tensor_tensor_reduce(row, row, s_b[0:n, b.ring(4), j], 1.0, 0.0, ALU.add, ALU.add, ln_b[0:n, b.ring(2), 1, j:j + 1])
                    ins.then_inc(x1_ready, 1)
                    wait(dve, x1_ready, b.n + 1)
                    v.tensor_scalar(ln_b[:, b.ring(2), 0], ln_b[:, b.ring(2), 1], -1.0 / C, None, ALU.mult).then_inc(mean_ready, 1)
                    weigh(b, (0,))
                b = s - 1
                if b.within(NB):
                    n, k = rows_of(b), b.ring(2)
                    wait(dve, q_exp, b.n + 1)
                    v.tensor_reduce(q_sum[0:n, k], q_e[0:n, k].rearrange("p (h d) -> p h d", d=DH), AX.X, ALU.add).then_inc(q_sums, 1)
                    wait(dve, q_sums, 2 * b.n + 1)
                    v.reciprocal(q_inv[0:n, k], q_sum[0:n, k]).then_inc(q_sums, 1)
                b = s - 4
                if b.within(NB):
                    weigh(b, (1,))
                b = s - 3
                if b.within(NB + 2):
                    if b.within(NB):
                        wait(dve, sumsq_ready, b.n + 1)
                    if (b - 2).within(NB):
                        wait(dve, var_ready, (b - 2).n + 1)
                    v.tensor_scalar(powb_in[:, s.ring(2), 1], varsum[:, (b - 2).ring(4)], 1.0 / C, LN_EPS, ALU.mult, ALU.add)
                    v.tensor_scalar(powb_in[:, s.ring(2), 0], sumsq[:, b.ring(4)], 1.0 / C, RMS_FLOOR ** 2 / C, ALU.mult, ALU.max).then_inc(powb_in_ready, 1)
                b = s - 4
                if b.within(NB):
                    lb_, cols = ln_b[:, b.ring(2)], bass.ds(b.n * J, J)
                    weigh(b, (2, 3)).then_inc(ln_step, 1)
                    wait(dve, ln_step, b.n + 1)
                    v.tensor_scalar(stat2[:, cols, 0], lb_[:, 0], -1.0, None, ALU.mult)
                    v.tensor_copy(dot2[:, cols], lb_[:, 6])

            def weigh(b, js):
                n = rows_of(b)
                for j in js:
                    ins = v.tensor_tensor_reduce(dot_junk[0:n, j], x1[0:n, b.ring(4), j], wr_r[0:n], 1.0, 0.0, ALU.mult, ALU.add, ln_b[0:n, b.ring(2), 6, j:j + 1])
                return ins

            v.memset(varsum, 1.0)
            v.memset(ln_b, 0.0)
            v.memset(powb_in, 1.0)
            v.memset(sumsq, 1.0)
            chain(v.memset(mix_r, 1.0))
            run_steps(dve, -2, LAST_B, *LOOP_B, step_b)

            dve.wait_ge(factors_ready, NB)
            for k in range(2):
                dve.wait_ge(o_stored[k], 16 * (NB // 2))
            mean, r = stat2[:, :, 0], stat2[:, :, 1]
            chain(v.tensor_scalar(t_cmp, mean, wr_sum[:, 0:1], None, ALU.mult))
            chain(v.tensor_tensor(t_cmp, dot2[:], t_cmp, ALU.subtract))
            chain(v.tensor_tensor(t_cmp, t_cmp, r, ALU.mult))
            chain(v.tensor_scalar(stat2[:, :, 2], t_cmp, br_c[:, 0:1], None, ALU.add))
            chain(v.memset(w_all, LOWEST))
            chain(v.tensor_copy(w_all[:, 0:COLS - J], stat2[:, 0:COLS - J, 2]))
            chain(v.tensor_copy(w_all[0:TAIL, COLS - J:COLS], stat2[0:TAIL, COLS - J:COLS, 2]))
            chain(v.tensor_scalar(t_rank, r, 1.0, None, ALU.add))
            chain(v.reciprocal(t_gt, t_rank))
            chain(v.tensor_tensor(t_rank, r, t_gt, ALU.mult))
            v.tensor_copy(stat2[:, :, 1], t_rank).then_inc(params_ready, 1)

            key, bit, mask, cand, fl, take, sgn = (small_i[:, k:k + 1] for k in range(7))
            cnt = small[:, 16:17]
            cnt3 = small[:, 32:35]
            cand3, fl3, unit3, take3 = (small_i[:, 8 + 3 * k:11 + 3 * k] for k in range(4))
            v.tensor_scalar(t_cmp, w_all, 0.0, None, ALU.is_ge, ALU.add, accum_out=cnt).then_inc(t_counts, 1)
            dve.wait_ge(t_total, 1)
            chain(v.tensor_scalar(sgn, psum[0][:, 0:1], K_SEL - 0.5, None, ALU.is_lt))
            chain(v.tensor_scalar(key, sgn, 31, None, ALU.logical_shift_left))
            chain(v.tensor_scalar(mask, sgn, 31, 31, ALU.logical_shift_left, ALU.arith_shift_right))
            chain(v.tensor_scalar(mask, mask, 0x7FFFFFFF, None, ALU.bitwise_and))
            chain(v.memset(take, 1))
            chain(v.tensor_scalar(bit, take, 30, None, ALU.logical_shift_left))
            chain(v.tensor_tensor(cand, key, bit, ALU.bitwise_or))
            chain(v.tensor_tensor(fl, cand, mask, ALU.bitwise_xor))
            v.tensor_scalar(t_cmp, w_all, fl.bitcast(F32), None, ALU.is_lt, ALU.add, accum_out=cnt).then_inc(t_counts, 1)
            dve.wait_ge(t_total, 2)
            few = P * COLS - K_SEL + 0.5
            chain(v.scalar_tensor_tensor(take, psum[0][:, 0:1], few, bit, ALU.is_lt, ALU.mult))
            chain(v.tensor_tensor(key, key, take, ALU.bitwise_or))
            for m in range(3):
                chain(v.memset(unit3[:, m:m + 1], m + 1))
            chain(v.tensor_scalar(unit3, unit3, 28, None, ALU.logical_shift_left))
            with dve.Fori(0, 5) as i:
                for r in range(3):
                    v.tensor_tensor(cand3, unit3, key.to_broadcast([P, 3]), ALU.bitwise_or).then_inc(t_step, 1)
                    wait(dve, t_step, i * 15 + (5 * r + 1))
                    v.tensor_tensor(fl3, cand3, mask.to_broadcast([P, 3]), ALU.bitwise_xor).then_inc(t_step, 1)
                    wait(dve, t_step, i * 15 + (5 * r + 2))
                    for m in range(3):
                        ins = v.tensor_scalar(t_cmp3[:, m], w_all, fl3[:, m:m + 1].bitcast(F32), None, ALU.is_lt, ALU.add, accum_out=cnt3[:, m:m + 1])
                    ins.then_inc(t_counts, 1)
                    wait(dve, t_total, i * 3 + (r + 3))
                    v.scalar_tensor_tensor(take3, psum[0][:, 0:3], few, unit3, ALU.is_lt, ALU.mult).then_inc(t_step, 1)
                    wait(dve, t_step, i * 15 + (5 * r + 3))
                    v.tensor_reduce(take, take3, AX.X, ALU.max).then_inc(t_step, 1)
                    v.tensor_scalar(unit3, unit3, 2, None, ALU.logical_shift_right).then_inc(t_step, 1)
                    wait(dve, t_step, i * 15 + (5 * r + 5))
                    v.tensor_tensor(key, key, take, ALU.bitwise_or).then_inc(t_key, 1)
                    wait(dve, t_key, i * 3 + (r + 1))
            chain(v.tensor_tensor(fl, key, mask, ALU.bitwise_xor))
            chain(v.tensor_scalar(t_eq, w_all, fl.bitcast(F32), None, ALU.is_equal))
            v.tensor_scalar(t_gt, w_all, fl.bitcast(F32), None, ALU.is_gt, ALU.add, accum_out=cnt).then_inc(t_counts, 1)
            dve.wait_ge(t_total, 18)
            chain(v.tensor_scalar(small[:, 18:19], psum[0][:, 0:1], -1.0, float(K_SEL), ALU.mult, ALU.add))
            ranks(t_eq, t_rank, t_rk, 2)
            chain(v.tensor_scalar(t_cmp, t_rank, small[:, 18:19], None, ALU.is_lt))
            chain(v.tensor_tensor(t_cmp, t_cmp, t_eq, ALU.mult))
            chain(v.tensor_tensor(t_sel, t_cmp, t_gt, ALU.add))
            ranks(t_sel, t_rank, t_rk, 3)
            chain(v.tensor_copy(t_ri[:, 0], t_rank))
            chain(v.tensor_scalar(t_ri[:, 1], t_ri[:, 0], 127, None, ALU.bitwise_and))
            chain(v.tensor_scalar(t_ri[:, 2], t_ri[:, 0], 7, None, ALU.logical_shift_right))
            chain(v.tensor_copy(t_lane, t_ri[:, 1]))
            chain(v.tensor_copy(t_fi, t_rk[:, 2]))
            chain(v.tensor_scalar(t_fi, t_fi, 7, None, ALU.logical_shift_right))
            chain(v.tensor_copy(t_first, t_fi))
            chain(v.tensor_copy(t_rel, t_ri[:, 2]))
            r3 = t_rel.rearrange("p (b j) -> p b j", j=J)
            chain(v.tensor_tensor(r3, r3, t_first.unsqueeze(2).to_broadcast([P, NB, J]), ALU.subtract))
            chain(v.tensor_scalar(t_rel, t_rel, 1.0, None, ALU.add))
            chain(v.tensor_tensor(t_rel, t_rel, t_sel, ALU.mult))
            chain(v.tensor_scalar(t_rel, t_rel, 1.0, None, ALU.subtract))
            chain(v.tensor_copy(t_ri[:, 0], iota_c[:, 0:COLS]))
            chain(v.tensor_scalar(t_ri[:, 0], t_ri[:, 0], J - 1, None, ALU.bitwise_and))
            chain(v.tensor_copy(j_pat, t_ri[:, 0]))
            chain(v.tensor_tensor(hot5[:, :, 0], t_rel.unsqueeze(2).to_broadcast([P, COLS, REL]), iota_c[:, 0:REL].unsqueeze(1).to_broadcast([P, COLS, REL]), ALU.is_equal))
            chain(v.tensor_scalar(hot5[:, :, 1], hot5[:, :, 0], lane_id[:, 0:1], None, ALU.mult))
            chain(v.tensor_tensor(hot5[:, :, 2], hot5[:, :, 0], j_pat.unsqueeze(2).to_broadcast([P, COLS, REL]), ALU.mult))

            def lanes(pr, k):
                v.tensor_tensor(hot_l[:, k], t_lane[:, bass.ds(pr * (2 * J), 2 * J)].unsqueeze(2).to_broadcast([P, 2 * J, P]),
                                iota_h[:, 0:P].unsqueeze(1).to_broadcast([P, 2 * J, P]), ALU.is_equal).then_inc(hotl_ready, 1)

            PEEL_T = 4 + NB // 2 % 4
            for pr in range(PEEL_T):
                wait(dve, hotl_used, pr - 3)
                lanes(pr, pr % 4)
            with dve.Fori(0, (NB // 2 - PEEL_T) // 4) as i:
                for k in range(4):
                    wait(dve, hotl_used, i * 4 + (PEEL_T + k - 3))
                    lanes(i * 4 + (PEEL_T + k), (PEEL_T + k) % 4)
            dve.wait_ge(hotl_used, NB // 2)
            chain(v.tensor_scalar(blk512, iota_c[:, 0:NB], float(BLOCK), None, ALU.mult))
            for q in range(-(-NB // PER)):
                n = min(PER, NB - q * PER)
                pp = psum[1 + q][:, 0:n * 3 * REL].rearrange("p (b k r) -> p k r b", k=3, r=REL)
                p1, p2 = part[:, :, q * PER:q * PER + n], part2[:, :, q * PER:q * PER + n]
                bb = blk512[:, q * PER:q * PER + n].unsqueeze(1).to_broadcast([P, REL, n])
                chain(v.tensor_tensor(p1, pp[:, 0], bb, ALU.mult))
                chain(v.tensor_scalar(p2, pp[:, 1], float(J), None, ALU.mult))
                chain(v.tensor_tensor(p1, p1, p2, ALU.add))
                chain(v.tensor_tensor(p1, p1, pp[:, 2], ALU.add))
            v.tensor_copy(small[:, 20:21], small[:, 18:19]).then_inc(part_ready, 1)
            dve.wait_ge(part_tr, 1)
            chain(v.tensor_copy(part_t[0:NB, 0:4], psum[6][0:NB, 0:4 * P].rearrange("p (r n) -> p r n", n=P)))
            chain(v.tensor_copy(part_t[0:NB, 4], psum[7][0:NB, 0:P]))
            chain(v.tensor_copy(first_c[0:NB], psum[7][0:NB, P:P + 1]))
            for k in range(REL):
                chain(v.tensor_scalar(small[0:NB, 24 + k:25 + k], first_c[0:NB], float(k), None, ALU.add))
                chain(v.tensor_scalar(place[0:NB, k], iota_c[0:NB, 0:LISTED], small[0:NB, 24 + k:25 + k], None, ALU.is_equal))
            v.tensor_copy(small[:, 21:22], small[:, 20:21]).then_inc(part_in, 1)
            chain(v.tensor_scalar(pad_far, iota_c[:, 0:LISTED], float(P), lane_id[:, 0:1], ALU.mult, ALU.add))
            chain(v.tensor_scalar(pad_far, pad_far, K_SEL - 0.5, FAR, ALU.is_gt, ALU.mult))
            dve.wait_ge(list_ps, 1)
            chain(v.tensor_tensor(list_keep[:], psum[5][:, 0:LISTED], pad_far, ALU.add))

            dve.wait_ge(ffn_ready, 1)
            v.memset(g_r[:, (NC - 1) % 4], 0.0)
            chain(v.memset(par[:, (NC - 1) % 4], 0.0))

            def step_c(s):
                b = s + 1
                if s.within(NC):
                    k = s.ring(2)
                    wait(dve, y_ps, (s - 1).of(2, 1))
                    for m in range(FK):
                        wait(dve, h_act, s.of(FK, 1) + m + 1)
                        v.tensor_copy(h_s[:, k, 0, m], h_f[:, m % 4]).then_inc(h_hi, 1)
                        wait(dve, h_hi, s.of(FK, 1) + m + 1)
                        v.tensor_tensor(h_s[:, k, 1, m], h_f[:, m % 4], h_s[:, k, 0, m], ALU.subtract).then_inc(h_lo, 1)
                        if m == FK // 2 - 1 and b.within(NC):
                            normalise_c(b)
                        if m == FK - 3 and (s + 2).within(NC):
                            columns_c(s + 2)
                else:
                    if (s + 2).within(NC):
                        columns_c(s + 2)
                    if b.within(NC):
                        normalise_c(b)
                if b.within(NC):
                    wait(dve, ct_ready, b.n + 1)
                    wait(dve, chi_ready, b.n + 1)
                    for h in range(2):
                        ins = v.tensor_tensor(xs_c[:, b.ring(2), 1, h], psum[h][:], xs_c[:, b.ring(2), 0, h], ALU.subtract)
                    ins.then_inc(clo_ready, 1)
                b = s - 1
                if b.within(NC):
                    for h in range(2):
                        finish_c(b, h)

            def columns_c(b):
                k = b.ring(4)
                wait(dve, scattered[k], b.of(16 * J, 4))
                v.tensor_copy(row_c[:, k], list_keep[:, bass.ds(b.n * J, J)]).then_inc(cols_c, 1)

            def normalise_c(b):
                k4, k = b.ring(4), b.ring(2)
                wait(dve, rows_in[k4], b.of(16 * J, 4) + 16 * J)
                wait(dve, pars_in[k4], b.of(16 * J, 4) + 16 * J)
                wait(dve, ct_ready, (b - 1).n)
                for j in range(J):
                    ins = v.tensor_scalar(ln_c[:, k, j], g_r[:, k4, j], par[:, k4, j, 0:1], par[:, k4, j, 1:2], ALU.subtract, ALU.mult)
                ins.then_inc(ln_ready, 1)
                for j in range(J):
                    v.scalar_tensor_tensor(g_r[:, k4, j], b2_r[:], par[:, k4, j, 2:3], g_r[:, k4, j], ALU.mult, ALU.add)

            def finish_c(b, h):
                k4 = b.ring(4)
                wait(dve, y_ps, b.of(2, 1) + h + 1)
                for j in (2 * h, 2 * h + 1):
                    row = g_r[:, k4, j]
                    ins = v.scalar_tensor_tensor(row, psum[6 + h][:, j % 2 * C:(j % 2 + 1) * C], par[:, k4, j, 2:3], row, ALU.mult, ALU.add)
                ins.then_inc(y_ready if h else y_half, 1)

            run_steps(dve, -2, NC, *LOOP_C, step_c)

        @block.tensor
        def _(pe):
            t_ = nc.tensor

            def mm(o, lhs, rhs, first, last):
                return t_.matmul(o, lhs, rhs, start=first, stop=last)

            def three(o, lhs, rhs, more=(), open_=True, close=True):
                n = 0
                todo = [(x, y, k) for k in range(2) for x, y in HI_LO]
                for x, y, k in todo:
                    ins = mm(o, lhs(x, k), rhs(y, k), open_ and n == 0, close and n == len(todo) - 1)
                    n += 1
                return ins

            def rank_totals(mask_sums, turn):
                pe.wait_ge(rank_in, turn)
                mm(psum[4][:, 0:NB], before[:], mask_sums, True, True)
                mm(psum[5][:, 0:NB], ones[:], mask_sums, True, True).then_inc(rank_sums, 1)

            pe.wait_ge(constants_ready, 3)

            def count_tile(k, ready, first, last):
                wait(pe, hot_ready, ready)
                ins = mm(psum[7][:, 0:COLS], hot_p[:, k], hot_c[:, k], first, last)
                ins.then_inc(counted if last else hot_used, 1)

            PEEL_E = 4 + NT % 4
            for t in range(PEEL_E):
                count_tile(t % 4, t + 1, t == 0, False)
            with pe.Fori(0, (NT - PEEL_E) // 4 - 1) as i:
                for k in range(4):
                    count_tile((PEEL_E + k) % 4, i * 4 + (PEEL_E + k + 1), False, False)
            for t in range(NT - 4, NT):
                count_tile(t % 4, t + 1, False, t == NT - 1)
            rank_totals(rk[:, 0], 1)
            pe.wait_ge(bias_act, 5)
            pe.wait_ge(weights_ready, 1)

            def step_a(s):
                b = s - 2
                if b.within(NB):
                    n = rows_of(b)
                    wait(pe, exp_ready, b.n + 1)
                    wait(pe, en_ready, (b).n)
                    for j in range(J):
                        ins = t_.transpose(psum[3][0:n, j * P:(j + 1) * P], e_t[:, b.ring(2), j * n:(j + 1) * n], ident[:])
                    ins.then_inc(et_ready, 1)
                b = s - 1
                if b.within(NB):
                    n = rows_of(b)
                    wait(pe, xhi_ready, b.n + 1)
                    wait(pe, xlo_ready, b.n + 1)
                    wait(pe, exp_ready, b.n)
                    three(psum[2][:, 0:n * J], lambda x, k: wk_s[:, x, k],
                          lambda y, k: xs_a[:, b.ring(2), y, k].rearrange("p (j r) -> p j r", j=J)[:, :, 0:n]).then_inc(keys_ready, 1)
                if s.within(NB):
                    n = rows_of(s)
                    wait(pe, normed, s.n + 1)
                    wait(pe, xlo_ready, s.n)
                    for k in range(2):
                        for j in range(J):
                            ins = t_.transpose(psum[k][:, j * P:j * P + n], xr[0:n, s.ring(4), j, k * P:(k + 1) * P], ident[0:n, 0:n])
                    ins.then_inc(xt_ready, 1)
                t = s
                if t.within(NT):
                    k = t.ring(2)
                    wait(pe, edge_cols, t.n + 1)
                    wait(pe, msg_ready, t.n)
                    t_.transpose(psum[5][:, 0:P], attr_c[:, k], ident[:]).then_inc(attr_tr, 1)
                    mm(psum[7][:, 0:P], ones[:], diag[:, k], True, True).then_inc(dst_row, 1)
                if t.within(NT):
                    wait(pe, attr_t_ready, t.n + 1)
                    mm(psum[5][:, 0:C], attr_t[0:RBF + 1, k], wd_f[:], True, True).then_inc(filter_ready, 1)
                t = s - 1
                if t.within(NT):
                    k = t.ring(2)
                    wait(pe, msg_ready, t.n + 1)
                    wait(pe, contrib_ready, t.n)
                    for h in range(2):
                        ins = mm(psum[6][:, h * P:(h + 1) * P], msg[:, k, h * P:(h + 1) * P], equal[:, k], True, True)
                    ins.then_inc(merged, 1)
                b = s - 2
                if b.within(NB):
                    n = rows_of(b)
                    wait(pe, en_ready, b.n + 1)
                    wait(pe, acc_step, b.n)
                    for j in range(J):
                        ins = mm(psum[4][:, 0:C], e_n[0:n, b.ring(2), j * P:(j + 1) * P], xr[0:n, b.ring(4), j], j == 0, j == J - 1)
                    ins.then_inc(sums_ready, 1)
                t = s - 1
                if t.within(NT):
                    k = t.ring(2)
                    wait(pe, merged_t, t.n + 1)
                    for h in range(2):
                        ins = mm(psum[6][:, C:2 * C], msg_t[:, k, h * P:(h + 1) * P], wb_f[:, h], h == 0, h == 1)
                    ins.then_inc(contrib_ps, 1)

            run_steps(pe, 0, NB + 1, *LOOP_A, step_a)

            pe.wait_ge(acc_step, NB)
            pe.wait_ge(xlo_ready, NB)
            pe.wait_ge(exp_ready, NB)
            pe.wait_ge(g_act, 1)
            for k in range(2):
                ins = t_.transpose(psum[0][:, k * P:(k + 1) * P], acc[:, k * P:(k + 1) * P], ident[:])
            ins.then_inc(g_ps, 1)
            t_.transpose(psum[1][0:MEM, 0:P], mem_e, ident[:])
            t_.transpose(psum[1][0:MEM, P:2 * P], mem_v[:], ident[:]).then_inc(g_ps, 1)
            pe.wait_ge(g_step, 3)
            for k in range(2):
                mm(psum[2][:, 0:P], wv_f[:, k], acc_t[:, k], k == 0, False)
            mm(psum[2][:, 0:P], mem_t[0:MEM, 1], mem_t[0:MEM, 0], False, True).then_inc(g_ps, 1)
            pe.wait_ge(g_step, 7)
            pe.wait_ge(en_ready, NB)
            mm(psum[3][:, 0:C], ctx_t, wo_f[:], True, True).then_inc(g_ps, 1)
            pe.wait_ge(stage_a_done, 1)

            def step_b(s):
                if s.within(NB):
                    n = rows_of(s)
                    wait(pe, xn_ready, s.n + 1)
                    wait(pe, blo_ready, s.n)
                    for k in range(2):
                        for j in range(J):
                            ins = t_.transpose(psum[k][:, j * P:j * P + n], xn[0:n, s.ring(2), j, k * P:(k + 1) * P], ident[0:n, 0:n])
                    ins.then_inc(xbt_ready, 1)
                b = s - 1
                if b.within(NB):
                    n, kk = rows_of(b), b.ring(2)
                    wait(pe, bhi_ready, b.n + 1)
                    wait(pe, blo_ready, b.n + 1)
                    wait(pe, qmax_step, b.of(2, 1))
                    for j in range(J):
                        ins = three(psum[2][0:n, j * P:(j + 1) * P], lambda x, k: xs_b[:, kk, x, k, j * P:j * P + n], lambda y, k: wq_s[:, y, k])
                    ins.then_inc(q_ready, 1)
                b = s - 3
                if b.within(NB):
                    n = rows_of(b)
                    wait(pe, qt_ready, b.n + 1)
                    wait(pe, mix_used, b.n)
                    for j in range(J):
                        o = psum[6 + j // 2][0:n, j % 2 * C:(j % 2 + 1) * C]
                        mm(o, q_t[:, b.ring(2), j * P:j * P + n], g_f[:], True, False)
                        ins = mm(o, ones_b[:, 0:n], bias_b[:, 1], False, True)
                    ins.then_inc(mix_ready, 1)
                b = s - 1
                if b.within(NB):
                    n, kk = rows_of(b), b.ring(2)
                    wait(pe, u_ready, b.n)
                    for j in range(J):
                        o = psum[4 + j // 2][0:n, j % 2 * C:(j % 2 + 1) * C]
                        three(o, lambda x, k: xs_b[:, kk, x, k, j * P:j * P + n], lambda y, k: wc_s[:, y, k], close=False)
                        ins = mm(o, ones_b[:, 0:n], bias_b[:, 0], False, True)
                    ins.then_inc(comb_ready, 1)
                b = s - 2
                if b.within(NB):
                    n = rows_of(b)
                    wait(pe, q_scaled, b.n + 1)
                    wait(pe, qt_ready, b.n)
                    for j in range(J):
                        ins = t_.transpose(psum[3][:, j * P:j * P + n], q_e[0:n, b.ring(2), j * P:(j + 1) * P], ident[0:n, 0:n])
                    ins.then_inc(qt_ps, 1)

            run_steps(pe, 0, NB + 2, *LOOP_B, step_b)

            pe.wait_ge(t_counts, 1)
            mm(psum[0][:, 0:1], ones[:], small[:, 16:17], True, True).then_inc(t_total, 1)
            pe.wait_ge(t_counts, 2)
            mm(psum[0][:, 0:1], ones[:], small[:, 16:17], True, True).then_inc(t_total, 1)
            with pe.Fori(0, 5) as i:
                for r in range(3):
                    wait(pe, t_counts, i * 3 + (r + 3))
                    mm(psum[0][:, 0:3], ones[:], small[:, 32:35], True, True).then_inc(t_total, 1)
            pe.wait_ge(t_counts, 18)
            mm(psum[0][:, 0:1], ones[:], small[:, 16:17], True, True).then_inc(t_total, 1)
            rank_totals(t_rk[:, 0], 2)
            rank_totals(t_rk[:, 0], 3)
            def gather_lists(q, pr, k, at):
                wait(pe, hotl_ready, pr + 1)
                for h in range(2):
                    for j in range(J):
                        ins = mm(psum[1 + q][:, bass.ds(at + h * 3 * REL, 3 * REL)], hot_l[:, k, h * J + j],
                                 hot5[:, bass.ds(pr * (2 * J) + (h * J + j), 1)].rearrange("p o k r -> p (o k r)"), j == 0, j == J - 1)
                ins.then_inc(hotl_used, 1)

            for q in range(-(-NB // PER)):
                pairs = min(PER, NB - q * PER) // 2
                first = q * PER // 2
                if pairs >= 4:
                    with pe.Fori(0, pairs // 4) as i:
                        for k in range(4):
                            gather_lists(q, i * 4 + (first + k), k, i * (24 * REL) + 6 * REL * k)
                for pr in range(pairs // 4 * 4, pairs):
                    gather_lists(q, first + pr, pr % 4, pr * 6 * REL)
            pe.wait_ge(part_ready, 1)
            for k in range(4):
                t_.transpose(psum[6][0:NB, k * P:(k + 1) * P], part[:, k], ident[:])
            t_.transpose(psum[7][0:NB, 0:P], part[:, 4], ident[:])
            t_.transpose(psum[7][0:NB, P:2 * P], t_first, ident[:]).then_inc(part_tr, 1)
            pe.wait_ge(part_in, 1)
            for k in range(REL):
                ins = mm(psum[5][:, 0:LISTED], part_t[0:NB, k], place[0:NB, k], k == 0, k == REL - 1)
            ins.then_inc(list_ps, 1)

            pe.wait_ge(ffn_ready, 1)
            def step_c(s):
                if s.within(NC):
                    kk = s.ring(2)
                    wait(pe, chi_ready, s.n + 1)
                    wait(pe, clo_ready, s.n + 1)
                    for m in range(FK):
                        wait(pe, h_act, s.of(FK, 1) + m - 3)
                        three(psum[2 + m % 4][:], lambda x, k: w1_s[:, x, k, m * P:(m + 1) * P], lambda y, k: xs_c[:, kk, y, k]).then_inc(h_ps, 1)
                b = s + 1
                if b.within(NC):
                    wait(pe, ln_ready, b.n + 1)
                    wait(pe, clo_ready, b.n)
                    for k in range(2):
                        for j in range(J):
                            ins = t_.transpose(psum[k][:, j * P:(j + 1) * P], ln_c[:, b.ring(2), j, k * P:(k + 1) * P], ident[:])
                    ins.then_inc(ct_ready, 1)
                b = s - 1
                if b.within(NC):
                    kk = b.ring(2)
                    wait(pe, h_lo, b.of(FK, 1) + FK)
                    for h in range(2):
                        wait(pe, y_half if h == 0 else y_ready, b.n)
                        for j in (2 * h, 2 * h + 1):
                            o = psum[6 + h][:, j % 2 * C:(j % 2 + 1) * C]
                            for m in range(FK):
                                for x, y in HI_LO:
                                    ins = mm(o, h_s[:, kk, x, m, j * P:(j + 1) * P], w2_s[:, y, m], m == 0 and (x, y) == (0, 0),
                                             m == FK - 1 and (x, y) == HI_LO[-1])
                        ins.then_inc(y_ps, 1)

            run_steps(pe, -1, NC, *LOOP_C, step_c)


NAMES = ["x", "src", "dst", "edge_attr_64", "edge_weight", "node_type_100", "L0_gnn_embed_table", "L0_gnn_W_dist", "L0_gnn_b_dist", "L0_gnn_W_comb",
         "L0_gnn_b_comb", "L0_mix_w_qkv", "L0_mix_mem_kv", "L0_mix_w_out", "L0_mix_b_out", "L0_mix_g_out", "L0_mix_g_pre", "L0_ffn_wr", "L0_ffn_br",
         "L0_ffn_w1", "L0_ffn_b1", "L0_ffn_w2", "L0_ffn_b2"]


def kernel(**inputs):
    import concourse.bacc as bacc
    from concourse.bass_utils import run_bass_kernel_spmd

    nc = bacc.Bacc("TRN2", target_bir_lowering=False, num_devices=1)
    arrays, args = {}, {}
    for name in NAMES:
        v = np.ascontiguousarray(inputs[name])
        arrays[f"in_{name}"] = v
        args[name] = nc.dram_tensor(f"in_{name}", v.shape, mybir.dt.from_np(v.dtype), kind="ExternalInput").ap()
    out = nc.dram_tensor("layer_out", inputs["x"].shape, F32, kind="ExternalOutput").ap()
    graph_layer(nc, args, out)
    return run_bass_kernel_spmd(nc, [arrays], core_ids=[0]).results[0]["layer_out"]
```
